# Optimizing a Trainium2 kernel written in Bass

```python
import numpy as np
import jax
import jax.numpy as jnp

def _softmax(x, axis=-1):
    return jax.nn.softmax(x, axis=axis)

def _gelu(x):
    return jax.nn.gelu(x, approximate=True)

def _silu(x):
    return jax.nn.silu(x)

def _sigmoid(x):
    return jax.nn.sigmoid(x)

def _layernorm(x, axis=-1, eps=1e-05):
    m = jnp.mean(x, axis=axis, keepdims=True)
    v = jnp.var(x, axis=axis, keepdims=True)
    return (x - m) / jnp.sqrt(v + eps)

def _scatter_add(tgt, idx, src, axis=0):
    return tgt.at[idx].add(src)

def _segment_sum(src, seg, n):
    return jax.ops.segment_sum(src, seg, n)
kernel_name = 'mk_gnn_ffn_d1_gnn_r32_7e50d7'

def setup_inputs(seed: int=0):
    np.random.seed(seed)
    _w = jnp.asarray

    def _rec_inputs():
        import jax
        import jax.numpy as jnp
        _gk = jax.random.key(seed)
        x = -0.0003713 + 1 * jax.random.normal(jax.random.fold_in(_gk, 1), (3125, 256), jnp.float32)
        src = jax.random.randint(jax.random.fold_in(_gk, 2), (50000,), 0, 3125, jnp.int32)
        dst = jax.random.randint(jax.random.fold_in(_gk, 3), (50000,), 0, 3125, jnp.int32)
        _o = jnp.argsort(dst, stable=True)
        src = src[_o]
        dst = dst[_o]
        return (x, src, dst)
    x, src, dst = _rec_inputs()

    def _L0_gnn_setup():
        import jax, jax.numpy as jnp
        import numpy as np
        N = 50000
        E = 25000
        F = 256
        BN_EPS = 1e-05

        def _gcn_conv(x, edge_index, W, b):
            n = x.shape[0]
            loops = jnp.arange(n, dtype=edge_index.dtype)
            row = jnp.concatenate([edge_index[0], loops])
            col = jnp.concatenate([edge_index[1], loops])
            deg = jax.ops.segment_sum(jnp.ones_like(col, dtype=x.dtype), col, num_segments=n)
            dinv = jnp.where(deg > 0, jax.lax.rsqrt(deg), 0.0)
            norm = dinv[row] * dinv[col]
            xw = x @ W
            msgs = norm[:, None] * xw[row]
            out = jax.ops.segment_sum(msgs, col, num_segments=n)
            return out + b
        key = jax.random.key(seed)
        ks = jax.random.split(key, 8)
        x = jax.random.normal(ks[0], (N, F), dtype=jnp.float32)
        edge_index = jax.random.randint(ks[1], (2, E), 0, N, dtype=jnp.int64)
        stdv = 1.0 / np.sqrt(F)
        conv_weight = jax.random.uniform(ks[2], (F, F), jnp.float32, -stdv, stdv)
        conv_bias = jax.random.uniform(ks[3], (F,), jnp.float32, -stdv, stdv)
        self_weight = jax.random.uniform(ks[4], (F, F), jnp.float32, -stdv, stdv)
        bias = jax.random.uniform(ks[5], (F,), jnp.float32, -stdv, stdv)
        gamma = jnp.ones((F,), jnp.float32)
        beta = jnp.zeros((F,), jnp.float32)
        return {'x': x, 'edge_index': edge_index, 'conv_weight': conv_weight, 'conv_bias': conv_bias, 'self_weight': self_weight, 'bias': bias, 'gamma': gamma, 'beta': beta}
    _L0_gnn_all = _L0_gnn_setup()
    _L0_gnn_in = {k: v for k, v in _L0_gnn_all.items() if k in ('conv_weight', 'conv_bias', 'self_weight', 'bias', 'gamma', 'beta')}
    del _L0_gnn_all

    def _L0_ffn_setup():
        import math
        import jax, jax.numpy as jnp
        import numpy as np
        CAPACITY_FACTOR = 1.25
        key = jax.random.key(seed)
        ks = jax.random.split(key, 5)
        B, L, D, F, E = (8, 256, 256, 1024, 8)
        h = jax.random.normal(ks[0], (B, L, D), dtype=jnp.float32)
        gate_w = jax.random.normal(ks[1], (D, E), dtype=jnp.float32) * 0.02
        gate_b = jnp.zeros((E,), dtype=jnp.float32)
        w1 = jax.random.normal(ks[2], (E, D, F), dtype=jnp.float32) * (1.0 / math.sqrt(D))
        b1 = jnp.zeros((E, F), dtype=jnp.float32)
        w2 = jax.random.normal(ks[3], (E, F, D), dtype=jnp.float32) * (1.0 / math.sqrt(F))
        b2 = jnp.zeros((E, D), dtype=jnp.float32)
        return {'h': h, 'gate_w': gate_w, 'gate_b': gate_b, 'w1': w1, 'b1': b1, 'w2': w2, 'b2': b2}
    _L0_ffn_all = _L0_ffn_setup()
    _L0_ffn_in = {k: v for k, v in _L0_ffn_all.items() if k in ('gate_w', 'gate_b', 'w1', 'b1', 'w2', 'b2')}
    del _L0_ffn_all
    return {'x': x, 'src': src, 'dst': dst, 'L0_gnn_conv_weight': _L0_gnn_in['conv_weight'], 'L0_gnn_conv_bias': _L0_gnn_in['conv_bias'], 'L0_gnn_self_weight': _L0_gnn_in['self_weight'], 'L0_gnn_bias': _L0_gnn_in['bias'], 'L0_gnn_gamma': _L0_gnn_in['gamma'], 'L0_gnn_beta': _L0_gnn_in['beta'], 'L0_ffn_gate_w': _L0_ffn_in['gate_w'], 'L0_ffn_gate_b': _L0_ffn_in['gate_b'], 'L0_ffn_w1': _L0_ffn_in['w1'], 'L0_ffn_b1': _L0_ffn_in['b1'], 'L0_ffn_w2': _L0_ffn_in['w2'], 'L0_ffn_b2': _L0_ffn_in['b2']}

def reference(x, src, dst, L0_gnn_conv_weight, L0_gnn_conv_bias, L0_gnn_self_weight, L0_gnn_bias, L0_gnn_gamma, L0_gnn_beta, L0_ffn_gate_w, L0_ffn_gate_b, L0_ffn_w1, L0_ffn_b1, L0_ffn_w2, L0_ffn_b2):
    import jax
    import jax.numpy as jnp

    def _L0_gnn_ref(x, edge_index, conv_weight, conv_bias, self_weight, bias, gamma, beta):
        import jax, jax.numpy as jnp
        import numpy as np
        N = 50000
        E = 25000
        F = 256
        BN_EPS = 1e-05

        def _gcn_conv(x, edge_index, W, b):
            n = x.shape[0]
            loops = jnp.arange(n, dtype=edge_index.dtype)
            row = jnp.concatenate([edge_index[0], loops])
            col = jnp.concatenate([edge_index[1], loops])
            deg = jax.ops.segment_sum(jnp.ones_like(col, dtype=x.dtype), col, num_segments=n)
            dinv = jnp.where(deg > 0, jax.lax.rsqrt(deg), 0.0)
            norm = dinv[row] * dinv[col]
            xw = x @ W
            msgs = norm[:, None] * xw[row]
            out = jax.ops.segment_sum(msgs, col, num_segments=n)
            return out + b
        out = _gcn_conv(x, edge_index, conv_weight, conv_bias)
        out = out + x @ self_weight
        out = out + bias
        mean = jnp.mean(out, axis=0)
        var = jnp.mean(jnp.square(out - mean), axis=0)
        out = (out - mean) * jax.lax.rsqrt(var + BN_EPS) * gamma + beta
        return jax.nn.relu(out) + x

    def _L0_ffn_ref(h, gate_w, gate_b, w1, b1, w2, b2):
        import math
        import jax, jax.numpy as jnp
        import numpy as np
        CAPACITY_FACTOR = 1.25
        B, L, D = h.shape
        E = gate_w.shape[1]
        T = B * L
        C = max(1, math.ceil(CAPACITY_FACTOR * T / E))
        x = h.reshape(T, D)
        logits = x @ gate_w + gate_b
        probs = jax.nn.softmax(logits, axis=-1)
        idx = jnp.argmax(probs, axis=-1)
        prb = jnp.take_along_axis(probs, idx[:, None], axis=1)[:, 0]
        one_hot = jax.nn.one_hot(idx, E, dtype=jnp.float32)
        pos = (jnp.cumsum(one_hot, axis=0) * one_hot).sum(-1).astype(jnp.int32) - 1
        kept = pos < C
        pos_safe = jnp.where(kept, pos, C)
        buf = jnp.zeros((E, C, D), dtype=h.dtype).at[idx, pos_safe].set(x, mode='drop')
        hmid = jax.nn.relu(jnp.einsum('ecd,edf->ecf', buf, w1) + b1[:, None, :])
        ybuf = jnp.einsum('ecf,efd->ecd', hmid, w2) + b2[:, None, :]
        pos_g = jnp.minimum(pos, C - 1)
        y_tok = ybuf[idx, pos_g] * (prb * kept)[:, None]
        y = y_tok.reshape(B, L, D)
        y = jnp.nan_to_num(y, nan=0.0, posinf=10000.0, neginf=-10000.0)
        return y
    edge_index = jnp.stack([src, dst])
    x = x + _L0_gnn_ref(_layernorm(x, axis=-1), edge_index, L0_gnn_conv_weight, L0_gnn_conv_bias, L0_gnn_self_weight, L0_gnn_bias, L0_gnn_gamma, L0_gnn_beta)
    x = x + _L0_ffn_ref(_layernorm(x, axis=-1)[None], L0_ffn_gate_w, L0_ffn_gate_b, L0_ffn_w1, L0_ffn_b1, L0_ffn_w2, L0_ffn_b2)[0]
    return x

_drawn_inputs = setup_inputs


def setup_inputs(seed=0):
    import zlib

    import numpy as np

    out = dict(_drawn_inputs(seed))
    spreads = {'L0_gnn_gamma': (1.0, 0.2),
     'L0_gnn_beta': (0.0, 0.1),
     'L0_ffn_gate_b': (0.0, 0.1),
     'L0_ffn_b1': (0.0, 0.8),
     'L0_ffn_b2': (0.0, 0.8)}
    factors = {'L0_gnn_conv_bias': 8.0, 'L0_gnn_bias': 8.0}
    for name, (base, spread) in spreads.items():
        noise = np.random.default_rng([zlib.crc32(name.encode()), seed]).standard_normal(out[name].shape)
        drawn = base * np.exp(spread * noise) if base else spread * noise
        out[name] = jnp.asarray(drawn.astype(out[name].dtype))
    for name, factor in factors.items():
        out[name] = (out[name] * factor).astype(out[name].dtype)
    return out
```

```python
from contextlib import ExitStack
from math import ceil

import concourse.bass as bass
from concourse import mybir

ALU = mybir.AluOpType
ACT = mybir.ActivationFunctionType
AX_X = mybir.AxisListType.X
F32 = mybir.dt.float32
BF16 = mybir.dt.bfloat16
I32 = mybir.dt.int32

NT = 25
MARGIN = 4
BATCH = 8
DPG = 2
XG = 5
EPS = 1e-5
ROUND = 12582912.0
NOWHERE = 1.0e6
FLT_MAX = 3.4028234663852886e38
CAPACITY_FACTOR = 1.25


def gnn_then_moe(nc, x, src, dst, conv_w, conv_b, self_w, self_b, gamma, beta,
                 gate_w, gate_b, w1, b1, w2, b2, out):
    N, D = x.shape
    E = src.shape[0]
    NX, _, F = w1.shape
    NP = N // NT
    NCH = E // NP
    CPT = NCH // NT
    WIN = CPT + 2 * MARGIN
    RING = 2 * CPT
    NB = WIN // BATCH
    KD = D // 128
    KF = F // 128
    CAP = max(1, ceil(CAPACITY_FACTOR * N / NX))
    SLOTS = 512
    SP4 = ceil(CAP / 4)
    SC = 4 * SP4
    TOK, PRB, RES = D, D + 1, D + 4
    ROW = RES + D
    GRP = 100
    NG = NCH // GRP
    TX = NT // XG
    DC = NCH // (XG * DPG)
    NDEG = XG * DPG
    assert NT * NP == N and NCH * NP == E and CPT * NT == NCH and SC <= SLOTS
    assert WIN % BATCH == 0 and MARGIN * 2 == BATCH and NT % 2 == 1 and NX % 2 == 0

    table = nc.dram_tensor("message_table", (N, D), F32).ap()
    slots = nc.dram_tensor("dispatched_rows", (NX * SLOTS, ROW), F32).ap()

    with ExitStack() as ctx:
        def sb(name, shape, dt=F32):
            return ctx.enter_context(nc.sbuf_tensor(name, shape, dt))

        def sem(name):
            return ctx.enter_context(nc.semaphore(name))

        Z = sb("Z", [NP, NT, D])
        XY = sb("XY", [NP, NT, ROW])
        Y = XY[:, :, 0:D]
        X = XY[:, :, RES:ROW]
        G = sb("G", [128, RING, D])
        OH = sb("OH", [NP, WIN, NP])
        WB = sb("WB", [128, 2, KD * F + KF * D])
        ident = sb("ident", [128, 128])
        ones = sb("ones", [NP, NP])
        upto = sb("upto", [NP, NP])
        lane = sb("lane", [NP, NP])
        lane_bf = sb("lane_bf", [NP, NP], BF16)
        tile0 = sb("tile0", [NP, NT])
        tokid = sb("tokid", [NP, NT])
        xid = sb("xid", [NP, NT, NX])
        eps = sb("eps", [128, 1])
        fills = sb("fills", [128, 3])
        wcs = sb("wcs", [128, KD, 2 * D])
        wg = sb("wg", [128, KD, NX])
        rows = sb("rows", [NP, 4, D])
        gbrow = sb("gbrow", [NP, NX])
        b1r = sb("b1r", [NX * KF, 128])
        b1c = sb("b1c", [128, NX * KF])
        b2row = sb("b2row", [SP4, NX, D])
        erow = sb("erow", [GRP, 2, NG, NP], I32)
        erow_f = sb("erow_f", [GRP, 2, NG, NP])
        dstT = sb("dstT", [NP, NCH])
        srcT = sb("srcT", [NP, NCH], I32)
        qf = sb("qf", [NP, NCH])
        rf = sb("rf", [NP, NCH])
        lo = sb("lo", [NP, NCH])
        hi = sb("hi", [NP, NCH])
        missing = sb("missing", [NP, 1])
        flag = sb("flag", [1, 1], I32)
        idx = sb("idx", [NP, RING], I32)
        dloc = sb("dloc", [NP, 2, WIN])
        stats = sb("stats", [NP, NT, 6])
        mv = sb("mv", [NP, NT, 2])
        std = sb("std", [NP, NT])
        rstd = sb("rstd", [NP, NT])
        dinv = sb("dinv", [NP, NT])
        h5 = sb("h5", [NP, TX, D])
        hT = sb("hT", [128, 2, KD, NP])
        fx_idx = sb("fx_idx", [NP, 1], I32)
        fx_loc = sb("fx_loc", [NP, NT])
        bnr = sb("bnr", [NP, 3, D])
        lg = sb("lg", [NP, NT, NX])
        pick = sb("pick", [NP, NT, NX])
        t8a = sb("t8a", [NP, NT, NX])
        t8b = sb("t8b", [NP, NT, NX])
        v25 = sb("v25", [NP, 6, NT])
        slot_i = sb("slot_i", [NP, NT], I32)
        tok_i = sb("tok_i", [SP4, 2, 4], I32)

        gbf = G[0:NP].rearrange("p a d -> p (a d)").bitcast(BF16)
        onr = gbf[:, 0:DPG * DC * NP].rearrange("p (b c n) -> p b c n", b=DPG, n=NP)
        onq = gbf[:, DPG * DC * NP:DPG * DC * (NP + NT)].rearrange("p (b c t) -> p b c t", b=DPG, t=NT)
        empty = OH[0:SP4].rearrange("p a d -> p (a d)")[:, 0:4 * ROW].rearrange("p (j c) -> p j c", j=4)
        gf = G[:].rearrange("p a d -> p (a d)")
        zf = Z[:].rearrange("p a d -> p (a d)")
        off = 2 * 4 * D
        hmid = gf[:, off:off + KF * SC].rearrange("p (f c) -> p f c", f=KF)
        off += KF * SC
        bufT = gf[:, off:off + KD * SC].rearrange("p (k c) -> p k c", k=KD)
        R = zf[0:SP4, 0:2 * 4 * ROW].rearrange("p (b j c) -> p b j c", b=2, j=4)
        yb = gf[0:SP4, 0:2 * 4 * D].rearrange("p (b j c) -> p b j c", b=2, j=4)
        mask = zf[0:SP4, 2 * 4 * ROW:2 * 4 * ROW + 4 * D].bitcast(I32)
        w1s = [WB[:, b, 0:KD * F].rearrange("p (k f) -> p k f", k=KD) for b in range(2)]
        w2s = [WB[:, b, KD * F:].rearrange("p (k d) -> p k d", k=KF) for b in range(2)]

        PS = ctx.enter_context(nc.psum_tensor("PS", [128, 8, 512], F32))

        dst_ld, src_ld = sem("dst_ld"), sem("src_ld")
        x_ld = [sem(f"x_ld{g}") for g in range(XG)]
        wcs_ld, rows_ld, gate_ld, b1_ld, b2_ld = (sem(s) for s in ("wcs_ld", "rows_ld", "gate_ld", "b1_ld", "b2_ld"))
        consts = sem("consts")
        passed = sem("passed")
        pool_step = sem("pool_step")
        dve_step = sem("dve_step")
        act_step = sem("act_step")
        erow_conv = sem("erow_conv")
        erow_turned = sem("erow_turned")
        src_ready = sem("src_ready")
        b1_turned, b1_ready = sem("b1_turned"), sem("b1_ready")
        empties_stored = sem("empties_stored")
        var_ready, std_ready, rstd_ready = sem("var_ready"), sem("std_ready"), sem("rstd_ready")
        h_ready, xh_ready, h_turned, hT_ready, xw_done, xw_copied = (
            sem(s) for s in ("h_ready", "xh_ready", "h_turned", "hT_ready", "xw_done", "xw_copied"))
        onehot_deg, deg_counted, degsqrt, dinv_ready = (
            sem(s) for s in ("onehot_deg", "deg_counted", "degsqrt", "dinv_ready"))
        y_scaled = [sem(f"y_scaled{g}") for g in range(XG)]
        table_stored = sem("table_stored")
        idx_staged = sem("idx_staged")
        gathered = [sem(f"gathered{s}") for s in range(RING)]
        missed, missed_sum, flag_ready = sem("missed"), sem("missed_sum"), sem("flag_ready")
        dloc_ready, onehots, batch_done, z_done, mean_summed = (
            sem(s) for s in ("dloc_ready", "onehots", "batch_done", "z_done", "mean_summed"))
        fx_staged, fx_gathered, fx_onehot, fx_mm, fx_added = (
            sem(s) for s in ("fx_staged", "fx_gathered", "fx_onehot", "fx_mm", "fx_added"))
        fx_remeaned, fx_located = sem("fx_remeaned"), sem("fx_located")
        ffn_half = sem("ffn_half")
        centred, squared, var_summed, bnstd, x2_ready = (
            sem(s) for s in ("centred", "squared", "var_summed", "bnstd", "x2_ready"))
        out_init = sem("out_init")
        var2_ready, std2_ready, h2_ready, h2_turned, h2T_ready, logits_done = (
            sem(s) for s in ("var2_ready", "std2_ready", "h2_ready", "h2_turned", "h2T_ready", "logits_done"))
        shifted, exped, picked, counted, slots_ready, scattered = (
            sem(s) for s in ("shifted", "exped", "picked", "counted", "slots_ready", "scattered"))
        w_ld = [sem(f"w_ld{b}") for b in range(2)]
        r_ld = [sem(f"r_ld{b}") for b in range(2)]
        r_turned, bufT_ready, hid_done, hid_ready, y_copied, y_ready = (
            sem(s) for s in ("r_turned", "bufT_ready", "hid_done", "hid_ready", "y_copied", "y_ready"))
        placed = [sem(f"placed{b}") for b in range(2)]

        NCONST = 12

        block = ctx.enter_context(nc.Block())

        def one(n):
            return bass.ds(n, 1)

        def hold(eng, s, n):
            eng.wait_ge(s, n)
            eng.sem_inc(passed, 1)

        def free(i, k):
            return TX * i + max(0, k - 1)

        @block.sync
        def _(sp):
            def edge_list(a):
                return a.rearrange("(k p j) -> p k j", k=NG, j=NP)

            sp.dma_start(erow[:, 0], edge_list(dst)).then_inc(dst_ld, 16)
            xt = x.rearrange("(t p) d -> p t d", p=NP)
            for g in range(XG):
                sp.dma_start(X[:, g * TX:(g + 1) * TX, :], xt[:, g * TX:(g + 1) * TX, :]).then_inc(x_ld[g], 16)
            sp.dma_start(erow[:, 1], edge_list(src)).then_inc(src_ld, 16)
            sp.wait_ge(consts, NCONST)
            for e in range(NX):
                sp.dma_start(slots[e * SLOTS:e * SLOTS + SC, :].rearrange("(p j) c -> p j c", j=4),
                             empty).then_inc(empties_stored, 16)
            tt = table.rearrange("(t p) d -> p t d", p=NP)
            for g in range(XG):
                sp.wait_ge(y_scaled[g], TX if g in (2, 3) else 1)
                sp.dma_start(tt[:, g * TX:(g + 1) * TX, :],
                             Y[:, g * TX:(g + 1) * TX, :]).then_inc(table_stored, 16)

            def weights(e, b):
                sp.dma_start(w1s[b], w1[one(e)].rearrange("a (k p) f -> p (a k) f", p=128)).then_inc(w_ld[b], 16)
                sp.dma_start(w2s[b], w2[one(e)].rearrange("a (k p) d -> p (a k) d", p=128)).then_inc(w_ld[b], 16)

            def tokens(e, b):
                sp.dma_start(R[:, b].rearrange("p j c -> p (j c)"),
                             slots[bass.ds(e * SLOTS, SC), :].rearrange("(p j) c -> p (j c)", j=4)).then_inc(r_ld[b], 16)

            for b in range(2):
                weights(b, b)
            ot = out.rearrange("(t p) d -> p t d", p=NP)
            for g in range(XG):
                sp.wait_ge(x2_ready, g + 1)
                sp.dma_start(ot[:, g * TX:(g + 1) * TX, :], X[:, g * TX:(g + 1) * TX, :]).then_inc(out_init, 16)
            sp.wait_ge(scattered, 16 * NT)
            for b in range(2):
                tokens(b, b)
            with sp.Fori(1, NX // 2) as i:
                for b in range(2):
                    sp.wait_ge(ffn_half, 2 * (2 * i + b - 1))
                    weights(2 * i + b, b)
                    sp.wait_ge(y_ready, 2 * i + b - 1)
                    tokens(2 * i + b, b)
            for b in range(2):
                sp.wait_ge(placed[b], 16 * 4 * (NX // 2))

        @block.gpsimd
        def _(pool):
            pool.memset(ident[:], 0.0).then_inc(pool_step, 1)
            pool.memset(upto[:], 1.0).then_inc(pool_step, 1)
            pool.memset(ones[:], 1.0).then_inc(consts, 1)
            pool.memset(eps[:], EPS).then_inc(consts, 1)
            pool.memset(empty, 0.0).then_inc(pool_step, 1)
            pool.iota(lane[:], [[1, NP]], base=0, channel_multiplier=0,
                      allow_small_or_imprecise_dtypes=True).then_inc(consts, 1)
            pool.iota(lane_bf[:], [[1, NP]], base=0, channel_multiplier=0,
                      allow_small_or_imprecise_dtypes=True).then_inc(consts, 1)
            pool.wait_ge(pool_step, 3)
            pool.affine_select(out=ident[:], in_=ident[:], compare_op=ALU.not_equal, fill=1.0, base=0,
                               pattern=[[-1, 128]], channel_multiplier=1).then_inc(consts, 1)
            pool.affine_select(out=upto[:], in_=upto[:], compare_op=ALU.is_ge, fill=0.0, base=0,
                               pattern=[[1, NP]], channel_multiplier=-1).then_inc(consts, 1)
            pool.memset(empty[:, :, TOK], NOWHERE).then_inc(consts, 1)
            pool.iota(tile0[:], [[NP, NT]], base=0, channel_multiplier=0,
                      allow_small_or_imprecise_dtypes=True).then_inc(consts, 1)
            pool.iota(tokid[:], [[NP, NT]], base=0, channel_multiplier=1,
                      allow_small_or_imprecise_dtypes=True).then_inc(consts, 1)
            pool.iota(xid[:], [[0, NT], [1, NX]], base=0, channel_multiplier=0,
                      allow_small_or_imprecise_dtypes=True).then_inc(consts, 1)
            lov = lo[:].rearrange("p (g r) -> p g r", r=CPT)
            hiv = hi[:].rearrange("p (g r) -> p g r", r=CPT)
            for v, r0, r1, base in ((lov, 0, MARGIN, -NP), (lov, MARGIN, CPT, 0),
                                    (hiv, 0, CPT - MARGIN, NP), (hiv, CPT - MARGIN, CPT, 2 * NP)):
                ins = pool.iota(v[:, :, r0:r1], [[NP, NT], [0, r1 - r0]], base=base, channel_multiplier=0,
                                allow_small_or_imprecise_dtypes=True)
            ins.then_inc(consts, 1)
            for c, v in enumerate((0.0, 1.0e4, -1.0e4)):
                ins = pool.memset(fills[:, c:c + 1], v)
            ins.then_inc(consts, 1)

            with pool.Fori(0, XG) as g:
                hold(pool, h_ready, TX * (g + 1))
                piece = X[:, bass.ds(TX * g, TX), :]
                pool.tensor_tensor(piece, piece, h5[:], ALU.add).then_inc(xh_ready, 1)

            pool.wait_ge(dinv_ready, 1)
            pool.wait_ge(xw_copied, 2 * NT)
            a, z = 4 * TX, 5 * TX
            pool.tensor_tensor(Y[:, a:z, :], Y[:, a:z, :],
                               dinv[:, a:z].unsqueeze(2).to_broadcast([NP, TX, D]), ALU.mult).then_inc(y_scaled[4], 1)

            pool.wait_ge(table_stored, 16 * XG)

            def gather_half(half, i):
                hold(pool, idx_staged, 2 * i + half + 1)
                for r in range(CPT):
                    s = half * CPT + r
                    if not isinstance(i, int):
                        if r == 0:
                            hold(pool, batch_done, NB * (2 * i - 2 + half) + 1)
                        if r == MARGIN:
                            hold(pool, batch_done, NB * (2 * i - 2 + half) + 2)
                        if r == CPT - MARGIN:
                            hold(pool, batch_done, NB * (2 * i - 2 + half + 1) + 1)
                    pool.indirect_dma_start(
                        out=G[0:NP, s, :], out_offset=None, in_=table,
                        in_offset=bass.IndirectOffsetOnAxis(ap=idx[:, s:s + 1], axis=0)).then_inc(gathered[s], 16)
            gather_half(0, 0)
            gather_half(1, 0)
            with pool.Fori(1, NT // 2) as i:
                gather_half(0, i)
                gather_half(1, i)
            last = NT // 2
            hold(pool, idx_staged, 2 * last + 1)
            for r in range(CPT):
                if r in (0, MARGIN):
                    hold(pool, batch_done, NB * (2 * last - 2) + 1 + r // MARGIN)
                if r == CPT - MARGIN:
                    hold(pool, batch_done, NB * (2 * last - 1) + 1)
                pool.indirect_dma_start(
                    out=G[0:NP, r, :], out_offset=None, in_=table,
                    in_offset=bass.IndirectOffsetOnAxis(ap=idx[:, r:r + 1], axis=0)).then_inc(gathered[r], 16)

            pool.wait_ge(flag_ready, 1)
            late = pool.value_load(flag[0:1, 0:1], min_val=0, max_val=E)
            with pool.If(late > 0):
                with pool.Fori(0, NCH) as c:
                    hold(pool, fx_staged, c + 1)
                    pool.indirect_dma_start(
                        out=G[0:NP, 0, :], out_offset=None, in_=table,
                        in_offset=bass.IndirectOffsetOnAxis(ap=fx_idx[:, 0:1], axis=0)).then_inc(fx_gathered, 16)

            for t in range(NT):
                if t == 0:
                    pool.wait_ge(slots_ready, 1)
                    pool.wait_ge(empties_stored, 16 * NX)
                pool.indirect_dma_start(
                    out=slots, out_offset=bass.IndirectOffsetOnAxis(ap=slot_i[:, t:t + 1], axis=0),
                    in_=XY[:, t, :], in_offset=None,
                    bounds_check=NX * SLOTS - 1, oob_is_err=False).then_inc(scattered, 16)

            pool.wait_ge(out_init, 16 * XG)
            with pool.Fori(0, NX // 2) as i:
                for b in range(2):
                    hold(pool, y_ready, 2 * i + b + 1)
                    for j in range(4):
                        pool.indirect_dma_start(
                            out=out, out_offset=bass.IndirectOffsetOnAxis(ap=tok_i[:, b, j:j + 1], axis=0),
                            in_=yb[:, b, j, :], in_offset=None,
                            bounds_check=N - 1, oob_is_err=False).then_inc(placed[b], 16)

        @block.scalar
        def _(act):
            for k in range(KD):
                act.dma_start(wcs[:, k, 0:D], conv_w[k * 128:(k + 1) * 128, :]).then_inc(wcs_ld, 16)
                act.dma_start(wcs[:, k, D:2 * D], self_w[k * 128:(k + 1) * 128, :]).then_inc(wcs_ld, 16)
            for c, v in enumerate((conv_b, self_b, gamma, beta)):
                act.dma_start(rows[:, c], v.rearrange("(a d) -> a d", a=1).to_broadcast([NP, D])).then_inc(rows_ld, 16)
            act.dma_start(wg[:], gate_w.rearrange("(k p) e -> p k e", p=128)).then_inc(gate_ld, 16)
            act.dma_start(gbrow[:], gate_b.rearrange("(a d) -> a d", a=1).to_broadcast([NP, NX])).then_inc(gate_ld, 16)
            act.dma_start(b1r[:], b1.rearrange("e (f p) -> (e f) p", p=128)).then_inc(b1_ld, 16)
            act.dma_start(b2row[:], b2.rearrange("(a e) d -> a e d", a=1).to_broadcast([SP4, NX, D])).then_inc(b2_ld, 16)

            act.wait_ge(consts, NCONST)
            for g in range(XG):
                act.wait_ge(var_ready, g + 1)
                act.activation(std[:, g * TX:(g + 1) * TX], mv[:, g * TX:(g + 1) * TX, 1], ACT.Sqrt,
                               bias=eps[0:NP, 0:1]).then_inc(std_ready, 1)

            def copy_hT(g, k):
                act.wait_ge(h_turned, TX * g + k + 1)
                act.wait_ge(xw_done, free(g, k))
                act.activation(hT[:, k % 2], PS[:, 3 + k % 2, 0:KD * NP].rearrange("p (k n) -> p k n", k=KD),
                               ACT.Copy).then_inc(hT_ready, 1)

            def copy_xw(g, k):
                act.wait_ge(xw_done, TX * g + k + 1)
                t = one(TX * g + k)
                act.activation(Y[:, t, :].rearrange("p a d -> p (a d)"), PS[0:NP, 5 + k % 2, 0:D],
                               ACT.Copy).then_inc(xw_copied, 1)
                act.activation(Z[:, t, :].rearrange("p a d -> p (a d)"), PS[0:NP, 5 + k % 2, D:2 * D],
                               ACT.Copy).then_inc(xw_copied, 1)
            with act.Fori(0, XG) as g:
                copy_hT(g, 0)
                for k in range(1, TX):
                    copy_hT(g, k)
                    copy_xw(g, k - 1)
                copy_xw(g, TX - 1)

            act.wait_ge(erow_turned, 2)
            act.activation(srcT[:], PS[0:NP, 1, 0:NCH], ACT.Copy).then_inc(src_ready, 1)
            act.wait_ge(b1_turned, 1)
            act.activation(b1c[:], PS[:, 7, 0:NX * KF], ACT.Copy).then_inc(b1_ready, 1)

            act.wait_ge(deg_counted, NDEG)
            act.activation(v25[:, 0], PS[0:NP, 2, 0:NT], ACT.Sqrt).then_inc(degsqrt, 1)
            act.wait_ge(dinv_ready, 1)
            for t in range(2 * TX, 4 * TX):
                act.activation(Y[:, t, :], Y[:, t, :], ACT.Copy, scale=dinv[:, t:t + 1]).then_inc(y_scaled[t // TX], 1)

            act.wait_ge(src_ready, 1)

            def stage(i, half, first=False):
                if not first:
                    for s in range(half * CPT, (half + 1) * CPT):
                        act.wait_ge(gathered[s], 16 * i)
                act.activation(idx[:, half * CPT:(half + 1) * CPT],
                               srcT[:, bass.ds(RING * i + half * CPT, CPT)], ACT.Copy).then_inc(idx_staged, 1)
            stage(0, 0, True)
            stage(0, 1, True)
            with act.Fori(1, NT // 2) as i:
                stage(i, 0)
                stage(i, 1)
            stage(NT // 2, 0)

            for g in range(XG):
                act.wait_ge(centred, g + 1)
                act.activation(Y[:, g * TX:(g + 1) * TX, :], Z[:, g * TX:(g + 1) * TX, :],
                               ACT.Square).then_inc(squared, 1)
            act.wait_ge(var_summed, 1)
            act.activation(bnr[:, 1], PS[0:NP, 3, 0:D], ACT.Sqrt, bias=eps[0:NP, 0:1],
                           scale=1.0 / N).then_inc(bnstd, 1)
            for g in range(XG):
                act.wait_ge(var2_ready, g + 1)
                act.activation(std[:, g * TX:(g + 1) * TX], mv[:, g * TX:(g + 1) * TX, 1], ACT.Sqrt,
                               bias=eps[0:NP, 0:1]).then_inc(std2_ready, 1)
            for t in range(NT):
                act.wait_ge(h2_turned, t + 1)
                if t >= 2:
                    act.wait_ge(logits_done, t - 1)
                act.activation(hT[:, t % 2], PS[:, 5 + t % 2, 0:KD * NP].rearrange("p (k n) -> p k n", k=KD),
                               ACT.Copy).then_inc(h2T_ready, 1)
            act.wait_ge(shifted, 1)
            act.activation(t8b[:], t8a[:], ACT.Exp).then_inc(exped, 1)

            act.wait_ge(b1_ready, 1)
            with act.Fori(0, NX) as e:
                act.wait_ge(r_turned, e + 1)
                act.activation(bufT, PS[:, 0:KD, 0:SC], ACT.Copy).then_inc(bufT_ready, 1)
                act.wait_ge(ffn_half, 2 * e)
                for f in range(KF):
                    act.wait_ge(hid_done, KF * e + f + 1)
                    act.activation(hmid[:, f], PS[:, 2 + f % 4, 0:SC], ACT.Relu,
                                   bias=b1c[:, one(KF * e + f)]).then_inc(hid_ready, 1)

        @block.tensor
        def _(pe):
            pe.wait_ge(consts, NCONST)
            idn = ident[0:NP, 0:NP]

            def turn_edges(which):
                pe.wait_ge(erow_conv, which + 1)
                for k in range(NG):
                    mm = pe.transpose(PS[0:NP, which, k * GRP:(k + 1) * GRP], erow_f[:, which, k],
                                      ident[0:GRP, 0:GRP])
                mm.then_inc(erow_turned, 1)
            turn_edges(0)

            def turn_h(g, k):
                pe.wait_ge(h_ready, TX * g + k + 1)
                pe.wait_ge(hT_ready, free(g, k))
                for c in range(KD):
                    mm = pe.transpose(PS[:, 3 + k % 2, c * NP:(c + 1) * NP], h5[:, k, c * 128:(c + 1) * 128], idn)
                mm.then_inc(h_turned, 1)

            def times_w(g, k):
                pe.wait_ge(hT_ready, TX * g + k + 1)
                pe.wait_ge(xw_copied, 2 * free(g, k))
                for c in range(KD):
                    mm = pe.matmul(PS[0:NP, 5 + k % 2], hT[:, k % 2, c], wcs[:, c], start=(c == 0), stop=(c == KD - 1))
                mm.then_inc(xw_done, 1)

            def count(g, b):
                pe.wait_ge(onehot_deg, DPG * g + b + 1)
                for k in range(DC):
                    mm = pe.matmul(PS[0:NP, 2, 0:NT], onr[:, b, k], onq[:, b, k],
                                   start=False, stop=False, skip_group_check=True)
                mm.then_inc(deg_counted, 1)
            pe.matmul(PS[0:NP, 2, 0:NT], ones[0:1, :], ones[0:1, 0:NT], start=True, stop=False, skip_group_check=True)
            pe.wait_ge(wcs_ld, 16 * 2 * KD)
            with pe.Fori(0, XG) as g:
                turn_h(g, 0)
                for k in range(TX):
                    if k + 1 < TX:
                        turn_h(g, k + 1)
                    times_w(g, k)
                for b in range(DPG):
                    count(g, b)
            turn_edges(1)
            pe.wait_ge(b1_ld, 16)
            pe.transpose(PS[:, 7, 0:NX * KF], b1r[:], ident[0:NX * KF, 0:NX * KF]).then_inc(b1_turned, 1)

            pe.wait_ge(missed, 1)
            pe.wait_ge(b1_ready, 1)
            pe.matmul(PS[0:1, 7, 0:1], ones[:, 0:1], missing[:], start=True, stop=True).then_inc(missed_sum, 1)
            pe.wait_ge(degsqrt, 1)

            def aggregate(t, par, start, skip, end, wraps):
                for b in range(NB):
                    pe.wait_ge(onehots, NB * t + b + 1)
                    for k in range(b * BATCH, (b + 1) * BATCH):
                        if k < skip or k >= end:
                            continue
                        c = start + k
                        pe.wait_ge(gathered[c % RING], 16 * (wraps + c // RING + 1))
                        if k == skip:
                            if not isinstance(t, int) or t >= 2:
                                pe.wait_ge(z_done, t - 1)
                        mm = pe.matmul(PS[0:NP, par, 0:D], OH[:, k], G[0:NP, c % RING, :],
                                       start=(k == skip), stop=(k == end - 1))
                    mm.then_inc(batch_done, 1)

            def sum_mean(t, start=False, stop=False):
                pe.wait_ge(z_done, t + 1)
                return pe.matmul(PS[0:NP, 2, 0:D], ones[:], Z[:, one(t), :].rearrange("p a d -> p (a d)"),
                                 start=start, stop=stop, skip_group_check=True)
            half = CPT - MARGIN
            aggregate(0, 0, -MARGIN, MARGIN, WIN, 0)
            aggregate(1, 1, half, 0, WIN, 0)
            sum_mean(0, start=True)
            with pe.Fori(1, NT // 2) as i:
                aggregate(2 * i, 0, -MARGIN, 0, WIN, i)
                sum_mean(2 * i - 1)
                aggregate(2 * i + 1, 1, half, 0, WIN, i)
                sum_mean(2 * i)
            aggregate(NT - 1, 0, -MARGIN, 0, CPT + MARGIN, NT // 2)
            sum_mean(NT - 2)
            sum_mean(NT - 1, stop=True).then_inc(mean_summed, 1)

            pe.wait_ge(flag_ready, 1)
            late = pe.value_load(flag[0:1, 0:1], min_val=0, max_val=E)
            with pe.If(late > 0):
                with pe.Fori(0, NCH) as c:
                    with pe.Fori(0, NT) as t:
                        pe.wait_ge(fx_gathered, 16 * (c + 1))
                        pe.wait_ge(fx_onehot, NT * c + t + 1)
                        pe.matmul(PS[0:NP, 4, 0:D], OH[:, 0], G[0:NP, 0, :], start=True, stop=True).then_inc(fx_mm, 1)
                pe.wait_ge(fx_added, NCH * NT)
                for t in range(NT):
                    mm = pe.matmul(PS[0:NP, 2, 0:D], ones[:], Z[:, t, :], start=(t == 0), stop=(t == NT - 1),
                                   skip_group_check=True)
                mm.then_inc(fx_remeaned, 1)

            for g in range(XG):
                pe.wait_ge(squared, g + 1)
                for t in range(g * TX, (g + 1) * TX):
                    mm = pe.matmul(PS[0:NP, 3, 0:D], ones[:], Y[:, t, :], start=(t == 0), stop=(t == NT - 1))
            mm.then_inc(var_summed, 1)

            pe.wait_ge(gate_ld, 32)

            def logits(t):
                pe.wait_ge(h2T_ready, t + 1)
                for k in range(KD):
                    mm = pe.matmul(PS[0:NP, 4, t * NX:(t + 1) * NX], hT[:, t % 2, k], wg[:, k],
                                   start=(k == 0), stop=(k == KD - 1))
                mm.then_inc(logits_done, 1)
            for t in range(NT):
                pe.wait_ge(h2_ready, t + 1)
                if t >= 2:
                    pe.wait_ge(h2T_ready, t - 1)
                for k in range(KD):
                    mm = pe.transpose(PS[:, 5 + t % 2, k * NP:(k + 1) * NP], Y[:, t, k * 128:(k + 1) * 128], idn)
                mm.then_inc(h2_turned, 1)
                if t >= 1:
                    logits(t - 1)
            logits(NT - 1)
            pe.wait_ge(picked, 1)
            pf = pick[:].rearrange("p t e -> p (t e)")
            pe.matmul(PS[0:NP, 0, 0:NT * NX], upto[:], pf, start=True, stop=True)
            pe.matmul(PS[0:NP, 1, 0:NT * NX], ones[:], pf, start=True, stop=True).then_inc(counted, 1)

            def expert(e, i, b):
                pe.wait_ge(r_ld[b], 16 * (i + 1))
                pe.wait_ge(bufT_ready, e)
                for j in range(4):
                    for k in range(KD):
                        mm = pe.transpose(PS[:, k, j * SP4:(j + 1) * SP4], R[:, b, j, k * 128:(k + 1) * 128],
                                          ident[0:SP4, 0:SP4])
                mm.then_inc(r_turned, 1)
                pe.wait_ge(w_ld[b], 32 * (i + 1))
                pe.wait_ge(bufT_ready, e + 1)
                for f in range(KF):
                    if f >= 4:
                        pe.wait_ge(hid_ready, KF * e + f - 3)
                    for k in range(KD):
                        mm = pe.matmul(PS[:, 2 + f % 4, 0:SC], w1s[b][:, k, f * 128:(f + 1) * 128], bufT[:, k],
                                       start=(k == 0), stop=(k == KD - 1))
                    mm.then_inc(hid_done, 1)
                pe.wait_ge(y_copied, 4 * e)
                for j in range(4):
                    for f in range(KF):
                        if j == 0:
                            pe.wait_ge(hid_ready, KF * e + f + 1)
                        mm = pe.matmul(PS[0:SP4, 6 + j // 2, (j % 2) * D:(j % 2 + 1) * D],
                                       hmid[:, f, j * SP4:(j + 1) * SP4], w2s[b][:, f],
                                       start=(f == 0), stop=(f == KF - 1))
                    if j % 2 == 1:
                        mm.then_inc(ffn_half, 1)
            with pe.Fori(0, NX // 2) as i:
                for b in range(2):
                    expert(2 * i + b, i, b)

        @block.vector
        def _(dve):
            done = [0]

            def link(ins):
                done[0] += 1
                ins.then_inc(dve_step, 1)
                dve.wait_ge(dve_step, done[0])

            def flat(a):
                return a.rearrange("p a d -> p (a d)")

            dve.wait_ge(dst_ld, 16)
            dve.tensor_copy(erow_f[:, 0], erow[:, 0]).then_inc(erow_conv, 1)

            def layer_stats(g, ready):
                for t in range(g * TX, (g + 1) * TX):
                    ins = dve.bn_stats(stats[:, t], X[:, t, :])
                link(ins)
                for t in range(g * TX, (g + 1) * TX):
                    ins = dve.bn_aggr(mv[:, t], stats[:, t])
                ins.then_inc(ready, 1)

            def layer_rstd(g, root):
                dve.wait_ge(root, g + 1)
                return dve.reciprocal(rstd[:, g * TX:(g + 1) * TX], std[:, g * TX:(g + 1) * TX])
            for g in range(XG):
                dve.wait_ge(x_ld[g], 16)
                layer_stats(g, var_ready)
                if g >= 1:
                    layer_rstd(g - 1, std_ready).then_inc(rstd_ready, TX)
            layer_rstd(XG - 1, std_ready).then_inc(rstd_ready, TX)
            dve.wait_ge(erow_turned, 1)
            link(dve.tensor_copy(dstT[:], PS[0:NP, 0, 0:NCH]))
            link(dve.tensor_scalar(qf[:], dstT[:], 1.0 / NP, 0.5 / NP - 0.5, ALU.mult, ALU.add))
            link(dve.tensor_scalar(rf[:], qf[:], ROUND, None, ALU.add))
            link(dve.tensor_scalar(qf[:], rf[:], ROUND, None, ALU.subtract))
            link(dve.scalar_tensor_tensor(out=rf[:], in0=qf[:], scalar=-float(NP), in1=dstT[:],
                                          op0=ALU.mult, op1=ALU.add))
            dve.wait_ge(consts, NCONST)
            dve.wait_ge(rstd_ready, NT)
            with dve.Fori(0, XG) as g:
                for k in range(TX):
                    if k == 0:
                        dve.wait_ge(h_turned, TX * g)
                        hold(dve, xh_ready, g)
                    t = TX * g + k
                    dve.tensor_scalar(h5[:, k], flat(X[:, one(t), :]), mv[:, one(t), 0], rstd[:, one(t)],
                                      ALU.subtract, ALU.mult).then_inc(h_ready, 1)
                for b in range(DPG):
                    dve.wait_ge(deg_counted, DPG * g)
                    c = DC * (DPG * g + b)
                    dve.tensor_tensor(onq[:, b], lane[:, 0:NT].unsqueeze(1).to_broadcast([NP, DC, NT]),
                                      qf[:, bass.ds(c, DC)].unsqueeze(2).to_broadcast([NP, DC, NT]), ALU.is_equal)
                    for k in range(DC):
                        ins = dve.tensor_scalar(onr[:, b, k], lane_bf[:], rf[:, one(c + k)], None, ALU.is_equal)
                    ins.then_inc(onehot_deg, 1)
            dve.wait_ge(src_ld, 16)
            dve.tensor_copy(erow_f[:, 1], erow[:, 1]).then_inc(erow_conv, 1)

            dve.wait_ge(degsqrt, 1)
            dve.reciprocal(dinv[:], v25[:, 0]).then_inc(dinv_ready, 1)
            dve.wait_ge(dinv_ready, 1)
            dve.wait_ge(xw_copied, 2 * NT)
            for g in range(2):
                a, z = g * TX, (g + 1) * TX
                dve.tensor_tensor(Y[:, a:z, :], Y[:, a:z, :], dinv[:, a:z].unsqueeze(2).to_broadcast([NP, TX, D]),
                                  ALU.mult).then_inc(y_scaled[g], 1)

            dve.wait_ge(rows_ld, 64)
            link(dve.tensor_tensor(bnr[:, 0], rows[:, 0], rows[:, 1], ALU.add))
            link(dve.tensor_tensor(Z[:], Z[:], bnr[:, 0].unsqueeze(1).to_broadcast([NP, NT, D]), ALU.add))
            for g in range(XG):
                dve.wait_ge(y_scaled[g], TX if g in (2, 3) else 1)
            for t in range(NT):
                ins = dve.scalar_tensor_tensor(out=Z[:, t, :], in0=Y[:, t, :], scalar=dinv[:, t:t + 1],
                                               in1=Z[:, t, :], op0=ALU.mult, op1=ALU.add)
            link(ins)

            link(dve.tensor_tensor(rf[:], dstT[:], lo[:], ALU.is_lt))
            link(dve.tensor_tensor(qf[:], dstT[:], hi[:], ALU.is_ge))
            link(dve.tensor_tensor(rf[:], rf[:], qf[:], ALU.add))
            dve.reduce_sum(missing[:], rf[:], axis=AX_X).then_inc(missed, 1)
            link(dve.scalar_tensor_tensor(out=qf[:], in0=dstT[:], scalar=1.0, in1=rf[:], op0=ALU.add, op1=ALU.mult))
            link(dve.tensor_scalar(qf[:], qf[:], -1.0, None, ALU.add))
            dve.wait_ge(missed_sum, 1)
            dve.tensor_copy(flag[:], PS[0:1, 7, 0:1]).then_inc(flag_ready, 1)

            link(dve.memset(XY[:, :, D:RES], 0.0))
            link(dve.tensor_copy(XY[:, :, TOK], tokid[:]))

            dve.wait_ge(empties_stored, 16 * NX)

            def onehot_tile(t, par, skip, end, first=False):
                n = end - skip
                dve.tensor_scalar(dloc[:, par, skip:end], dstT[:, bass.ds(CPT * t - MARGIN + skip, n)],
                                  tile0[:, one(t)], None, ALU.subtract).then_inc(dloc_ready, 1)
                dve.wait_ge(dloc_ready, t + 1)
                for b in range(NB):
                    if not first:
                        dve.wait_ge(batch_done, NB * (t - 1) + b + 1)
                    for k in range(max(skip, b * BATCH), min(end, (b + 1) * BATCH)):
                        ins = dve.tensor_scalar(OH[:, k], lane[:], dloc[:, par, k:k + 1], None, ALU.is_equal)
                    ins.then_inc(onehots, 1)

            def finish_tile(t, par):
                dve.wait_ge(batch_done, NB * (t + 1))
                dve.scalar_tensor_tensor(out=flat(Z[:, one(t), :]), in0=PS[0:NP, par, 0:D], scalar=dinv[:, one(t)],
                                         in1=flat(Z[:, one(t), :]), op0=ALU.mult, op1=ALU.add).then_inc(z_done, 1)
            onehot_tile(0, 0, MARGIN, WIN, first=True)
            onehot_tile(1, 1, 0, WIN)
            finish_tile(0, 0)
            with dve.Fori(1, NT // 2) as i:
                onehot_tile(2 * i, 0, 0, WIN)
                finish_tile(2 * i - 1, 1)
                onehot_tile(2 * i + 1, 1, 0, WIN)
                finish_tile(2 * i, 0)
            onehot_tile(NT - 1, 0, 0, CPT + MARGIN)
            finish_tile(NT - 2, 1)
            finish_tile(NT - 1, 0)
            dve.wait_ge(z_done, NT)

            late = dve.value_load(flag[0:1, 0:1], min_val=0, max_val=E)
            with dve.If(late > 0):
                with dve.Fori(0, NCH) as c:
                    dve.tensor_scalar(fx_loc[:], tile0[:], -1.0, qf[:, one(c)], ALU.mult, ALU.add) \
                       .then_inc(fx_located, 1)
                    dve.tensor_copy(fx_idx[:], srcT[:, one(c)]).then_inc(fx_staged, 1)
                    with dve.Fori(0, NT) as t:
                        dve.wait_ge(fx_located, c + 1)
                        dve.tensor_scalar(OH[:, 0], lane[:], fx_loc[:, one(t)], None, ALU.is_equal) \
                           .then_inc(fx_onehot, 1)
                        dve.wait_ge(fx_mm, NT * c + t + 1)
                        dve.scalar_tensor_tensor(out=flat(Z[:, one(t), :]), in0=PS[0:NP, 4, 0:D],
                                                 scalar=dinv[:, one(t)], in1=flat(Z[:, one(t), :]),
                                                 op0=ALU.mult, op1=ALU.add).then_inc(fx_added, 1)
                        dve.wait_ge(fx_added, NT * c + t + 1)
                dve.wait_ge(fx_remeaned, 1)

            dve.wait_ge(mean_summed, 1)
            link(dve.tensor_scalar(bnr[:, 0], PS[0:NP, 2, 0:D], 1.0 / N, None, ALU.mult))

            def row(c):
                return bnr[:, c].unsqueeze(1).to_broadcast([NP, TX, D])
            for g in range(XG):
                a, z = g * TX, (g + 1) * TX
                dve.tensor_tensor(Z[:, a:z, :], Z[:, a:z, :], row(0), ALU.subtract).then_inc(centred, 1)
            dve.wait_ge(centred, XG)
            dve.wait_ge(bnstd, 1)
            link(dve.reciprocal(bnr[:, 2], bnr[:, 1]))
            link(dve.tensor_tensor(bnr[:, 2], bnr[:, 2], rows[:, 2], ALU.mult))
            for g in range(XG):
                a, z = g * TX, (g + 1) * TX
                dve.wait_ge(squared, g + 1)
                link(dve.tensor_tensor(Z[:, a:z, :], Z[:, a:z, :], row(2), ALU.mult))
                link(dve.tensor_tensor(Z[:, a:z, :], Z[:, a:z, :],
                                       rows[:, 3].unsqueeze(1).to_broadcast([NP, TX, D]), ALU.add))
                dve.scalar_tensor_tensor(out=X[:, a:z, :], in0=Z[:, a:z, :], scalar=0.0, in1=X[:, a:z, :],
                                         op0=ALU.max, op1=ALU.add).then_inc(x2_ready, 1)
                dve.wait_ge(x2_ready, g + 1)
                layer_stats(g, var2_ready)

                def normalise(g):
                    link(layer_rstd(g, std2_ready))
                    for t in range(g * TX, (g + 1) * TX):
                        dve.tensor_scalar(Y[:, t, :], X[:, t, :], mv[:, t, 0:1], rstd[:, t:t + 1],
                                          ALU.subtract, ALU.mult).then_inc(h2_ready, 1)
                if g >= 1:
                    normalise(g - 1)
            normalise(XG - 1)

            logit = PS[0:NP, 4, 0:NT * NX].rearrange("p (t e) -> p t e", e=NX)
            best, total, prob, chosen, place, kept = (v25[:, c] for c in range(6))

            def wide(a):
                return a.unsqueeze(2).to_broadcast([NP, NT, NX])
            dve.wait_ge(logits_done, NT)
            link(dve.tensor_tensor(lg[:], logit, gbrow[:].unsqueeze(1).to_broadcast([NP, NT, NX]), ALU.add))
            link(dve.tensor_reduce(best, lg[:], AX_X, ALU.max))
            dve.tensor_tensor(t8a[:], lg[:], wide(best), ALU.subtract).then_inc(shifted, 1)
            link(dve.tensor_tensor(pick[:], lg[:], wide(best), ALU.is_equal))
            link(dve.tensor_scalar(lg[:], xid[:], -1.0, float(NX), ALU.mult, ALU.add))
            link(dve.tensor_tensor(lg[:], lg[:], pick[:], ALU.mult))
            link(dve.tensor_reduce(chosen, lg[:], AX_X, ALU.max))
            dve.tensor_tensor(pick[:], lg[:], wide(chosen), ALU.is_equal).then_inc(picked, 1)
            dve.wait_ge(exped, 1)
            link(dve.tensor_reduce(total, t8b[:], AX_X, ALU.add))
            link(dve.reciprocal(prob, total))
            link(dve.tensor_copy(XY[:, :, PRB], prob))

            dve.wait_ge(counted, 1)
            link(dve.memset(t8a[:, 0], 0.0))
            link(dve.tensor_copy(t8a[:, 1:NT], PS[0:NP, 1, 0:(NT - 1) * NX].rearrange("p (t e) -> p t e", e=NX)))
            now, then = t8a, t8b
            step = 1
            while step < NT:
                dve.tensor_copy(then[:, 0:step], now[:, 0:step])
                link(dve.tensor_tensor(then[:, step:NT], now[:, step:NT], now[:, 0:NT - step], ALU.add))
                now, then = then, now
                step *= 2
            link(dve.tensor_tensor(now[:], now[:], PS[0:NP, 0, 0:NT * NX].rearrange("p (t e) -> p t e", e=NX), ALU.add))
            link(dve.tensor_tensor(now[:], now[:], pick[:], ALU.mult))
            link(dve.tensor_reduce(place, now[:], AX_X, ALU.add))
            link(dve.tensor_scalar(kept, place, float(CAP), None, ALU.is_le))
            link(dve.tensor_scalar(kept, kept, -NOWHERE, NOWHERE, ALU.mult, ALU.add))
            link(dve.scalar_tensor_tensor(out=place, in0=chosen, scalar=-float(SLOTS), in1=place,
                                          op0=ALU.mult, op1=ALU.add))
            link(dve.tensor_scalar(place, place, float(NX * SLOTS - 1), None, ALU.add))
            dve.tensor_tensor(slot_i[:], place, kept, ALU.add).then_inc(slots_ready, 1)

            dve.wait_ge(b2_ld, 16)
            base, LINKS = done[0], 8
            with dve.Fori(0, NX // 2) as i:
                for b in range(2):
                    e = 2 * i + b
                    n = 0

                    def then(ins):
                        nonlocal n
                        n += 1
                        ins.then_inc(dve_step, 1)
                        hold(dve, dve_step, LINKS * e + (base + n))
                    dve.wait_ge(r_ld[b], 16 * (i + 1))
                    dve.wait_ge(placed[b], 64 * i)
                    then(dve.tensor_copy(tok_i[:, b], R[:, b, :, TOK]))
                    for j in range(4):
                        if j % 2 == 0:
                            dve.wait_ge(ffn_half, 2 * e + j // 2 + 1)
                        dve.tensor_tensor(yb[:, b, j], PS[0:SP4, 6 + j // 2, (j % 2) * D:(j % 2 + 1) * D],
                                          flat(b2row[:, one(e), :]), ALU.add).then_inc(y_copied, 1)
                    dve.wait_ge(y_copied, 4 * e + 4)
                    for j in range(4):
                        ins = dve.tensor_scalar(yb[:, b, j], yb[:, b, j], R[:, b, j, PRB:PRB + 1], None, ALU.mult)
                    then(ins)
                    yf = yb[:, b].rearrange("p j d -> p (j d)")
                    then(dve.tensor_tensor(mask, yf, yf, ALU.not_equal))
                    then(dve.copy_predicated(yf, mask, fills[0:SP4, 0:1].to_broadcast([SP4, 4 * D])))
                    then(dve.tensor_scalar(mask, yf, FLT_MAX, None, ALU.is_gt))
                    then(dve.copy_predicated(yf, mask, fills[0:SP4, 1:2].to_broadcast([SP4, 4 * D])))
                    then(dve.tensor_scalar(mask, yf, -FLT_MAX, None, ALU.is_lt))
                    then(dve.copy_predicated(yf, mask, fills[0:SP4, 2:3].to_broadcast([SP4, 4 * D])))
                    dve.tensor_tensor(yb[:, b], yb[:, b], R[:, b, :, RES:ROW], ALU.add).then_inc(y_ready, 1)
                    assert n == LINKS


INPUTS = ["x", "src", "dst", "L0_gnn_conv_weight", "L0_gnn_conv_bias", "L0_gnn_self_weight", "L0_gnn_bias",
          "L0_gnn_gamma", "L0_gnn_beta", "L0_ffn_gate_w", "L0_ffn_gate_b", "L0_ffn_w1", "L0_ffn_b1",
          "L0_ffn_w2", "L0_ffn_b2"]


def kernel(**inputs):
    import numpy as np
    import concourse.bacc as bacc
    from concourse.bass_utils import run_bass_kernel_spmd

    nc = bacc.Bacc("TRN2", target_bir_lowering=False, num_devices=1)
    arrays, args = {}, []
    for name in INPUTS:
        a = np.ascontiguousarray(inputs[name])
        arrays[f"in_{name}"] = a
        args.append(nc.dram_tensor(f"in_{name}", a.shape, mybir.dt.from_np(a.dtype), kind="ExternalInput").ap())
    shape = arrays["in_x"].shape
    args.append(nc.dram_tensor("out", shape, F32, kind="ExternalOutput").ap())
    gnn_then_moe(nc, *args)
    r = run_bass_kernel_spmd(nc, [arrays], core_ids=[0])
    return r.results[0]["out"]
```

```python
from contextlib import ExitStack
from math import ceil

import concourse.bass as bass
from concourse import mybir

ALU = mybir.AluOpType
ACT = mybir.ActivationFunctionType
AX_X = mybir.AxisListType.X
F32 = mybir.dt.float32
F32R = mybir.dt.float32r
BF16 = mybir.dt.bfloat16
I32 = mybir.dt.int32

NT = 25
MARGIN = 4
BATCH = 8
DPG = 2
TB = 4
XG = 5
EPS = 1e-5
ROUND = 12582912.0
NOWHERE = 1.0e6
FLT_MAX = 3.4028234663852886e38
CAPACITY_FACTOR = 1.25
INFINITE = 1.0e4
T_BANKS = (5, 6, 7, 0)
L_BANKS = (4, 1)


def gnn_then_moe(nc, x, src, dst, conv_w, conv_b, self_w, self_b, gamma, beta,
                 gate_w, gate_b, w1, b1, w2, b2, out):
    N, D = x.shape
    E = src.shape[0]
    NX, _, F = w1.shape
    NP = N // NT
    NCH = E // NP
    CPT = NCH // NT
    WIN = CPT + 2 * MARGIN
    RING = 2 * CPT
    NB = WIN // BATCH
    KD = D // 128
    KF = F // 128
    CAP = max(1, ceil(CAPACITY_FACTOR * N / NX))
    SLOTS = 512
    SP4 = ceil(CAP / 4)
    SC = 4 * SP4
    TOK, PRB, RES = D, D + 1, D + 4
    ROW = RES + D
    GRP = 100
    NG = NCH // GRP
    HALVES = ((0, KD * F), (KD * F, KD * F + KF * D))
    BN_POOL = (XG - 2, XG - 1)
    ROUTES = ((0, 3 * NT // XG), (3 * NT // XG, NT))
    TX = NT // XG
    DC = NCH // (XG * DPG)
    NDEG = XG * DPG
    assert NT * NP == N and NCH * NP == E and CPT * NT == NCH and SC <= SLOTS
    assert WIN % BATCH == 0 and MARGIN * 2 == BATCH and NT % 2 == 1 and NX % 2 == 0

    table = nc.dram_tensor("message_table", (N, D), F32).ap()
    slots = nc.dram_tensor("dispatched_rows", (NX * SLOTS, ROW), F32).ap()

    with ExitStack() as ctx:
        def sb(name, shape, dt=F32):
            return ctx.enter_context(nc.sbuf_tensor(name, shape, dt))

        def sem(name):
            return ctx.enter_context(nc.semaphore(name))

        FB = 4
        part_a, part_b, part_c, part_d = 52 * 1024, NT * D * FB, RING * D * FB, 12 * 1024
        part_e = 2 * (KD * F + KF * D) * FB
        part_f = (KD * F + KF * D) * FB
        arena_at = ceil(nc.sbuf_base / 32) * 32
        sb("arena", [128, (part_a + part_b + part_c + part_d + part_e + part_f) // FB])

        class Part:

            def __init__(self, start, size):
                self.at, self.end = arena_at + start, arena_at + start + size

            def place(self, name, shape, dt=F32):
                size = 2 if dt == BF16 else 4
                for n in shape[1:]:
                    size *= n
                t = nc.alloc_sbuf_tensor_at(name, shape, dt, offset=self.at)
                self.at += ceil(size / 32) * 32
                assert self.at <= self.end, name
                return t

        starts = [0, part_a, part_a + part_b, part_a + part_b + part_c, part_a + part_b + part_c + part_d,
                  part_a + part_b + part_c + part_d + part_e]

        def part(n):
            return Part(starts[n], (part_a, part_b, part_c, part_d, part_e, part_f)[n])

        XY = part(0).place("XY", [NP, NT, ROW])
        Y = XY[:, :, 0:D]
        X = XY[:, :, RES:ROW]
        Z = part(1).place("Z", [NP, NT, D])
        G = part(2).place("G", [NP, RING, D])
        OH = part(3).place("OH", [NP, WIN, NP])
        p = part(2)
        onr = p.place("onr", [NP, DPG, NP, DC], BF16)
        onq = p.place("onq", [NP, DPG, NT, DC], BF16)
        p = part(4)
        wcs = p.place("wcs", [128, KD, 2 * D])
        lanes = p.place("lanes", [NP, NP, DC], BF16)
        erow = p.place("erow", [GRP, 2, NG, NP], I32)
        erow_f = p.place("erow_f", [GRP, 2, NG, NP])
        h5 = p.place("h5", [NP, TX, D])
        lo = p.place("lo", [NP, NCH])
        hi = p.place("hi", [NP, NCH])
        raw = part(5).place("raw", [128, KD * F + KF * D])
        w_hi, w_lo = [], []
        for b, p in enumerate((part(4), part(0))):
            w_hi.append(p.place(f"w_hi{b}", [128, KD * F + KF * D], F32R))
            w_lo.append(p.place(f"w_lo{b}", [128, KD * F + KF * D], F32R))
        b2row = p.place("b2row", [SP4, NX, D])
        hid = p.place("hid", [128, 2, SC])
        fin_a = p.place("fin_a", [SP4, 4 * D])
        p = part(1)
        R = p.place("R", [SP4, 2, 4, D])
        tail = p.place("tail", [SP4, 2, 4, ROW - D])
        yb = p.place("yb", [SP4, 2, 4, D])
        p = part(2)
        hid_hi = p.place("hid_hi", [128, KF, SC], F32R)
        hid_lo = p.place("hid_lo", [128, KF, SC], F32R)
        p = part(3)
        buf_hi = p.place("buf_hi", [128, KD, SC], F32R)
        buf_lo = p.place("buf_lo", [128, KD, SC], F32R)
        fin_b = p.place("fin_b", [SP4, 4 * D])

        def w1_of(a):
            return a[:, 0:KD * F].rearrange("p (k f) -> p k f", k=KD)

        def w2_of(a):
            return a[:, KD * F:].rearrange("p (k d) -> p k d", k=KF)

        empty = sb("empty", [SP4, 1, ROW])
        ident = sb("ident", [128, 128])
        ones = sb("ones", [NP, NP])
        upper = sb("upper", [NP, NP])
        lane = sb("lane", [NP, NP])
        tile0 = sb("tile0", [NP, NT])
        tokid = sb("tokid", [NP, NT])
        xid = sb("xid", [NP, NT, NX])
        eps = sb("eps", [128, 1])
        wg = sb("wg", [128, KD, NX])
        rows = sb("rows", [NP, 4, D])
        gbrow = sb("gbrow", [NP, NX])
        b1r = sb("b1r", [NX * KF, 128])
        b1c = sb("b1c", [128, NX * KF])
        dstT = sb("dstT", [NP, NCH])
        srcT = sb("srcT", [NP, NCH], I32)
        qf = sb("qf", [NP, NCH])
        rf = sb("rf", [NP, NCH])
        q_bf = sb("q_bf", [NP, NCH], BF16)
        r_bf = sb("r_bf", [NP, NCH], BF16)
        missing = sb("missing", [NP, 1])
        flag = sb("flag", [1, 1], I32)
        idx = sb("idx", [NP, RING], I32)
        dloc = sb("dloc", [NP, 2, WIN])
        stats = sb("stats", [NP, NT, 6])
        mv = sb("mv", [NP, NT, 2])
        std = sb("std", [NP, NT])
        rstd = sb("rstd", [NP, NT])
        nmr = sb("nmr", [NP, NT])
        rstd1 = sb("rstd1", [NP, NT])
        sqdeg = sb("sqdeg", [NT, NP])
        dinv = sb("dinv", [NP, NT])
        hT = sb("hT", [128, TB, KD, NP])
        dev = sb("dev", [NP, 2, 2, D])
        fx_idx = sb("fx_idx", [NP, 1], I32)
        fx_loc = sb("fx_loc", [NP, NT])
        nought = sb("nought", [NP, NP])
        shift = sb("shift", [NP, D])
        bnr = sb("bnr", [NP, 4, D])
        lg = sb("lg", [NP, NT, NX])
        pick = sb("pick", [NP, NT, NX])
        t8a = sb("t8a", [NP, NT, NX])
        t8b = sb("t8b", [NP, NT, NX])
        carry = sb("carry", [NP, NX])
        v25 = sb("v25", [NP, 6, NT])
        slot_i = sb("slot_i", [NP, NT], I32)
        tok_i = sb("tok_i", [SP4, 2, 4], I32)

        PS = ctx.enter_context(nc.psum_tensor("PS", [128, 8, 512], F32))

        dst_ld, src_ld = sem("dst_ld"), sem("src_ld")
        z_biased, own_added = sem("z_biased"), sem("own_added")
        x_ld = [sem(f"x_ld{g}") for g in range(XG)]
        wcs_ld, rows_ld, gate_ld, b1_ld, b2_ld = (sem(s) for s in ("wcs_ld", "rows_ld", "gate_ld", "b1_ld", "b2_ld"))
        consts, ident_ready, lanes_ready = sem("consts"), sem("ident_ready"), sem("lanes_ready")
        passed = sem("passed")
        pool_step = sem("pool_step")
        dve_step = sem("dve_step")
        act_step = sem("act_step")
        erow_conv = sem("erow_conv")
        erow_turned = sem("erow_turned")
        src_ready = sem("src_ready")
        b1_turned, b1_ready = sem("b1_turned"), sem("b1_ready")
        empties_stored = sem("empties_stored")
        var_ready, std_ready, rstd_ready = sem("var_ready"), sem("std_ready"), sem("rstd_ready")
        h_ready, xh_ready, h_turned, hT_ready, xw_done, xw_copied = (
            sem(s) for s in ("h_ready", "xh_ready", "h_turned", "hT_ready", "xw_done", "xw_copied"))
        onehot_deg, deg_counted, degsqrt, degsqrt_turned, dinv_ready = (
            sem(s) for s in ("onehot_deg", "deg_counted", "degsqrt", "degsqrt_turned", "dinv_ready"))
        y_scaled = [sem(f"y_scaled{g}") for g in range(XG)]
        table_stored = sem("table_stored")
        idx_staged = sem("idx_staged")
        gathered = [sem(f"gathered{s}") for s in range(RING)]
        missed, missed_sum, flag_ready = sem("missed"), sem("missed_sum"), sem("flag_ready")
        dloc_ready, onehots, batch_done, z_done = (
            sem(s) for s in ("dloc_ready", "onehots", "batch_done", "z_done"))
        fx_staged, fx_gathered, fx_onehot, fx_mm, fx_added = (
            sem(s) for s in ("fx_staged", "fx_gathered", "fx_onehot", "fx_mm", "fx_added"))
        fx_located, fx_dev, fx_squared, fx_summed = (
            sem(s) for s in ("fx_located", "fx_dev", "fx_squared", "fx_summed"))
        tile_summed, shift_ready, dev_ready, squared, dev_summed, bn_scale, bnstd, bn_rows, bn_part, x2_ready = (
            sem(s) for s in ("tile_summed", "shift_ready", "dev_ready", "squared", "dev_summed", "bn_scale", "bnstd",
                             "bn_rows", "bn_part", "x2_ready"))
        out_init = sem("out_init")
        var2_ready, std2_ready, nmr_ready, h2_ready, h2_turned, h2T_ready, logits_done = (
            sem(s) for s in ("var2_ready", "std2_ready", "nmr_ready", "h2_ready", "h2_turned", "h2T_ready",
                             "logits_done"))
        shifted, exped, picked, counted, slots_ready, scattered = (
            sem(s) for s in ("shifted", "exped", "picked", "counted", "slots_ready", "scattered"))
        raw_ld = [sem(f"raw_ld{half}") for half in range(2)]
        w_hi_ready, w_lo_ready = sem("w_hi_ready"), sem("w_lo_ready")
        r_ld = [sem(f"r_ld{b}") for b in range(2)]
        tail_ld = [sem(f"tail_ld{b}") for b in range(2)]
        r_turned, buf_hi_ready, buf_lo_ready, hid_done, hid_relu, hid_hi_ready, hid_lo_ready = (
            sem(s) for s in ("r_turned", "buf_hi_ready", "buf_lo_ready", "hid_done", "hid_relu", "hid_hi_ready",
                             "hid_lo_ready"))
        ffn_done, y_copied, y_ready, yb_free = (sem(s) for s in ("ffn_done", "y_copied", "y_ready", "yb_free"))
        placed = [sem(f"placed{b}") for b in range(2)]

        NCONST = 9

        block = ctx.enter_context(nc.Block())

        def one(n):
            return bass.ds(n, 1)

        def hold(eng, s, n):
            eng.wait_ge(s, n)
            eng.sem_inc(passed, 1)

        def past(n):
            return n + 1

        def free(g, k):
            return TX * g + max(0, k - 1)

        @block.sync
        def _(sp):
            def edge_list(a):
                return a.rearrange("(k p j) -> p k j", k=NG, j=NP)

            sp.dma_start(erow[:, 0], edge_list(dst)).then_inc(dst_ld, 16)
            xt = x.rearrange("(t p) d -> p t d", p=NP)
            for g in range(XG):
                sp.dma_start(X[:, g * TX:(g + 1) * TX, :], xt[:, g * TX:(g + 1) * TX, :]).then_inc(x_ld[g], 16)
                if g == 0:
                    sp.dma_start(erow[:, 1], edge_list(src)).then_inc(src_ld, 16)

            def weights(e, first=False):
                sources = (w1[one(e)].rearrange("a (k p) f -> p (a k) f", p=128),
                           w2[one(e)].rearrange("a (k p) d -> p (a k) d", p=128))
                for half, (place, source) in enumerate(zip((w1_of(raw), w2_of(raw)), sources)):
                    if not first:
                        sp.wait_ge(w_hi_ready, 2 * e - 1 + half)
                        sp.wait_ge(w_lo_ready, 2 * e - 1 + half)
                    sp.dma_start(place, source).then_inc(raw_ld[half], 16)

            def load_rows(e, b):
                sp.dma_start(R[:, b], slots[bass.ds(e * SLOTS, SC), 0:D]
                             .rearrange("(p j) c -> p j c", j=4)).then_inc(r_ld[b], 16)

            def load_tail(e, b):
                sp.dma_start(tail[:, b], slots[bass.ds(e * SLOTS, SC), D:ROW]
                             .rearrange("(p j) c -> p j c", j=4)).then_inc(tail_ld[b], 16)

            weights(0, True)
            sp.wait_ge(consts, NCONST)
            for e in range(NX):
                sp.dma_start(slots[e * SLOTS:e * SLOTS + SC, :].rearrange("(p j) c -> p j c", j=4),
                             empty[:].to_broadcast([SP4, 4, ROW])).then_inc(empties_stored, 16)
            tt = table.rearrange("(t p) d -> p t d", p=NP)
            for g in range(XG):
                sp.wait_ge(y_scaled[g], TX if g in (2, 3) else 1)
                sp.dma_start(tt[:, g * TX:(g + 1) * TX, :],
                             Y[:, g * TX:(g + 1) * TX, :]).then_inc(table_stored, 16)
            weights(1)
            ot = out.rearrange("(t p) d -> p t d", p=NP)
            for g in range(XG):
                sp.wait_ge(x2_ready, g + 1)
                sp.dma_start(ot[:, g * TX:(g + 1) * TX, :], X[:, g * TX:(g + 1) * TX, :]).then_inc(out_init, 16)
            sp.wait_ge(scattered, 16 * NT)
            for b in range(2):
                load_rows(b, b)
            for b in range(2):
                load_tail(b, b)
            sp.wait_ge(out_init, 16 * XG)
            sp.dma_start(b2row[:], b2.rearrange("(a e) d -> a e d", a=1).to_broadcast([SP4, NX, D])).then_inc(b2_ld, 16)

            def inputs(e, b):
                sp.wait_ge(r_turned, e - 1)
                load_rows(e, b)
                weights(e)

            def tokens(e, i, b):
                sp.wait_ge(y_ready, e - 1)
                load_tail(e, b)
                sp.wait_ge(placed[b], 64 * i)
                sp.sem_inc(yb_free, 1)
            inputs(2, 0)
            with sp.Fori(1, NX // 2 - 1) as i:
                inputs(2 * i + 1, 1)
                tokens(2 * i, i, 0)
                inputs(2 * i + 2, 0)
                tokens(2 * i + 1, i, 1)
            inputs(NX - 1, 1)
            for b in range(2):
                tokens(NX - 2 + b, NX // 2 - 1, b)
            for b in range(2):
                sp.wait_ge(placed[b], 16 * 4 * (NX // 2))

        @block.gpsimd
        def _(pool):
            pool.memset(ident[:], 0.0).then_inc(pool_step, 1)
            pool.memset(upper[:], 1.0).then_inc(pool_step, 1)
            pool.memset(ones[:], 1.0).then_inc(consts, 1)
            pool.memset(eps[:], EPS).then_inc(consts, 1)
            pool.wait_ge(pool_step, 2)
            pool.affine_select(out=ident[:], in_=ident[:], compare_op=ALU.not_equal, fill=1.0, base=0,
                               pattern=[[-1, 128]], channel_multiplier=1).then_inc(ident_ready, 1)
            pool.affine_select(out=upper[:], in_=upper[:], compare_op=ALU.is_ge, fill=0.0, base=0,
                               pattern=[[1, NP]], channel_multiplier=-1).then_inc(consts, 1)
            pool.iota(lanes[:], [[1, NP], [0, DC]], base=0, channel_multiplier=0,
                      allow_small_or_imprecise_dtypes=True).then_inc(lanes_ready, 1)
            pool.iota(lane[:], [[1, NP]], base=0, channel_multiplier=0,
                      allow_small_or_imprecise_dtypes=True).then_inc(consts, 1)
            pool.memset(empty[:], 0.0).then_inc(pool_step, 1)
            pool.iota(tile0[:], [[NP, NT]], base=0, channel_multiplier=0,
                      allow_small_or_imprecise_dtypes=True).then_inc(consts, 1)
            pool.iota(tokid[:], [[NP, NT]], base=0, channel_multiplier=1,
                      allow_small_or_imprecise_dtypes=True).then_inc(consts, 1)
            pool.iota(xid[:], [[0, NT], [1, NX]], base=0, channel_multiplier=0,
                      allow_small_or_imprecise_dtypes=True).then_inc(consts, 1)
            lov = lo[:].rearrange("p (g r) -> p g r", r=CPT)
            hiv = hi[:].rearrange("p (g r) -> p g r", r=CPT)
            for v, r0, r1, base in ((lov, 0, MARGIN, -NP), (lov, MARGIN, CPT, 0),
                                    (hiv, 0, CPT - MARGIN, NP), (hiv, CPT - MARGIN, CPT, 2 * NP)):
                ins = pool.iota(v[:, :, r0:r1], [[NP, NT], [0, r1 - r0]], base=base, channel_multiplier=0,
                                allow_small_or_imprecise_dtypes=True)
            ins.then_inc(consts, 1)
            pool.wait_ge(pool_step, 3)
            pool.memset(empty[:, :, TOK], NOWHERE).then_inc(consts, 1)

            pool.wait_ge(dinv_ready, 1)
            pool.wait_ge(xw_copied, past(NT))
            a, z = 4 * TX, 5 * TX
            pool.tensor_tensor(Y[:, a:z, :], Y[:, a:z, :],
                               dinv[:, a:z].unsqueeze(2).to_broadcast([NP, TX, D]), ALU.mult).then_inc(y_scaled[4], 1)

            pool.wait_ge(table_stored, 16 * XG)

            def gather_half(half, i):
                hold(pool, idx_staged, 2 * i + half + 1)
                for r in range(CPT):
                    s = half * CPT + r
                    if not isinstance(i, int):
                        if r == 0:
                            hold(pool, batch_done, NB * (2 * i - 2 + half) + 1)
                        if r == MARGIN:
                            hold(pool, batch_done, NB * (2 * i - 2 + half) + 2)
                        if r == CPT - MARGIN:
                            hold(pool, batch_done, NB * (2 * i - 2 + half + 1) + 1)
                    pool.indirect_dma_start(
                        out=G[:, s, :], out_offset=None, in_=table,
                        in_offset=bass.IndirectOffsetOnAxis(ap=idx[:, s:s + 1], axis=0)).then_inc(gathered[s], 16)
            gather_half(0, 0)
            gather_half(1, 0)
            with pool.Fori(1, NT // 2) as i:
                gather_half(0, i)
                gather_half(1, i)
            last = NT // 2
            hold(pool, idx_staged, 2 * last + 1)
            for r in range(CPT):
                if r in (0, MARGIN):
                    hold(pool, batch_done, NB * (2 * last - 2) + 1 + r // MARGIN)
                if r == CPT - MARGIN:
                    hold(pool, batch_done, NB * (2 * last - 1) + 1)
                pool.indirect_dma_start(
                    out=G[:, r, :], out_offset=None, in_=table,
                    in_offset=bass.IndirectOffsetOnAxis(ap=idx[:, r:r + 1], axis=0)).then_inc(gathered[r], 16)

            pool.wait_ge(flag_ready, 1)
            late = pool.value_load(flag[0:1, 0:1], min_val=0, max_val=E)
            with pool.If(late > 0):
                with pool.Fori(0, NCH) as c:
                    hold(pool, fx_staged, c + 1)
                    pool.indirect_dma_start(
                        out=G[:, 0, :], out_offset=None, in_=table,
                        in_offset=bass.IndirectOffsetOnAxis(ap=fx_idx[:, 0:1], axis=0)).then_inc(fx_gathered, 16)

            pool.wait_ge(bn_rows, 1)
            for g in BN_POOL:
                piece = Z[:, g * TX:(g + 1) * TX, :]
                pool.tensor_tensor(piece, piece, bnr[:, 2].unsqueeze(1).to_broadcast([NP, TX, D]),
                                   ALU.mult).then_inc(pool_step, 1)
                pool.wait_ge(pool_step, 4 + g - BN_POOL[0])
                pool.tensor_tensor(piece, piece, bnr[:, 3].unsqueeze(1).to_broadcast([NP, TX, D]),
                                   ALU.add).then_inc(bn_part, 1)

            for n, (t0, t1) in enumerate(ROUTES):
                pool.wait_ge(slots_ready, n + 1)
                pool.wait_ge(h2_ready, t1)
                for t in range(t0, t1):
                    if t == 0:
                        pool.wait_ge(empties_stored, 16 * NX)
                    pool.indirect_dma_start(
                        out=slots, out_offset=bass.IndirectOffsetOnAxis(ap=slot_i[:, t:t + 1], axis=0),
                        in_=XY[:, t, :], in_offset=None,
                        bounds_check=NX * SLOTS - 1, oob_is_err=False).then_inc(scattered, 16)

            pool.wait_ge(scattered, 16 * NT)
            pool.wait_ge(out_init, 16 * XG)

            def low_parts(e, b):
                for half, (a, z) in enumerate(HALVES):
                    hold(pool, w_hi_ready, 2 * e + half + 1)
                    pool.tensor_tensor(w_lo[b][:, a:z], raw[:, a:z], w_hi[b][:, a:z].bitcast(F32),
                                       ALU.subtract).then_inc(w_lo_ready, 1)

            def place_rows(e, b):
                hold(pool, y_ready, e + 1)
                for j in range(4):
                    pool.indirect_dma_start(
                        out=out, out_offset=bass.IndirectOffsetOnAxis(ap=tok_i[:, b, j:j + 1], axis=0),
                        in_=yb[:, b, j, :], in_offset=None,
                        bounds_check=N - 1, oob_is_err=False).then_inc(placed[b], 16)
            low_parts(1, 1)
            with pool.Fori(1, NX // 2) as i:
                for b in range(2):
                    low_parts(2 * i + b, b)
                    place_rows(2 * i - 2 + b, b)
            place_rows(NX - 2, 0)
            place_rows(NX - 1, 1)

        @block.scalar
        def _(act):
            for k in range(KD):
                act.dma_start(wcs[:, k, 0:D], conv_w[k * 128:(k + 1) * 128, :]).then_inc(wcs_ld, 16)
                act.dma_start(wcs[:, k, D:2 * D], self_w[k * 128:(k + 1) * 128, :]).then_inc(wcs_ld, 16)
            for c, v in enumerate((conv_b, self_b, gamma, beta)):
                act.dma_start(rows[:, c], v.rearrange("(a d) -> a d", a=1).to_broadcast([NP, D])).then_inc(rows_ld, 16)
            act.dma_start(wg[:], gate_w.rearrange("(k p) e -> p k e", p=128)).then_inc(gate_ld, 16)
            act.dma_start(gbrow[:], gate_b.rearrange("(a d) -> a d", a=1).to_broadcast([NP, NX])).then_inc(gate_ld, 16)
            act.dma_start(b1r[:], b1.rearrange("e (f p) -> (e f) p", p=128)).then_inc(b1_ld, 16)
            for s in (hT_ready, xw_copied):
                act.sem_inc(s, 1)

            act.wait_ge(consts, NCONST)
            for g in range(XG):
                act.wait_ge(var_ready, g + 1)
                act.activation(std[:, g * TX:(g + 1) * TX], mv[:, g * TX:(g + 1) * TX, 1], ACT.Sqrt,
                               bias=eps[0:NP, 0:1]).then_inc(std_ready, 1)

            def copy_hT(g, k):
                act.wait_ge(h_turned, past(TX * g + k + 1))
                act.wait_ge(xw_done, past(free(g, k)))
                act.activation(hT[:, k % 2], PS[:, 3 + k % 2, 0:KD * NP].rearrange("p (k n) -> p k n", k=KD),
                               ACT.Copy).then_inc(hT_ready, 1)

            def copy_xw(g, k):
                act.wait_ge(xw_done, past(TX * g + k + 1))
                act.activation(Y[:, one(TX * g + k), :].rearrange("p a d -> p (a d)"), PS[0:NP, 5 + k % 2, 0:D],
                               ACT.Copy).then_inc(xw_copied, 1)
            with act.Fori(0, XG) as g:
                copy_hT(g, 0)
                for k in range(1, TX):
                    copy_hT(g, k)
                    copy_xw(g, k - 1)
                copy_xw(g, TX - 1)

            def layernorm(g, first, k):
                act.wait_ge(h_turned, past(TX * (g - 1) + k + 1))
                t = one(first + k)
                act.activation(h5[:, k], X[:, t, :].rearrange("p a d -> p (a d)"), ACT.Identity, bias=nmr[:, t],
                               scale=rstd[:, t]).then_inc(h_ready, 1)
            act.wait_ge(nmr_ready, 1)
            for k in range(TX):
                layernorm(XG, 0, k)

            act.wait_ge(erow_turned, 2)
            act.activation(srcT[:], PS[0:NP, 1, 0:NCH], ACT.Copy).then_inc(src_ready, 1)
            act.wait_ge(b1_turned, 1)
            act.activation(b1c[:], PS[:, 7, 0:NX * KF], ACT.Copy).then_inc(b1_ready, 1)

            act.wait_ge(deg_counted, DPG + NDEG)
            act.activation(sqdeg[:], PS[0:NT, 2, 0:NP], ACT.Sqrt).then_inc(degsqrt, 1)
            act.wait_ge(dinv_ready, 1)
            for t in range(2 * TX, 4 * TX):
                act.activation(Y[:, t, :], Y[:, t, :], ACT.Copy, scale=dinv[:, t:t + 1]).then_inc(y_scaled[t // TX], 1)

            act.wait_ge(src_ready, 1)

            def stage(i, half, first=False):
                if not first:
                    for s in range(half * CPT, (half + 1) * CPT):
                        act.wait_ge(gathered[s], 16 * i)
                act.activation(idx[:, half * CPT:(half + 1) * CPT],
                               srcT[:, bass.ds(RING * i + half * CPT, CPT)], ACT.Copy).then_inc(idx_staged, 1)
            stage(0, 0, True)
            stage(0, 1, True)

            def copy_self(g, first, k):
                act.wait_ge(xw_done, past(TX * g + k + 1))
                act.activation(Z[:, one(first + k), :].rearrange("p a d -> p (a d)"), PS[0:NP, 5 + k % 2, 0:D],
                               ACT.Copy).then_inc(xw_copied, 1)

            def second_lap(g, first, last=False):
                for k in range(TX):
                    copy_hT(g, k)
                    if k >= 1:
                        copy_self(g, first, k - 1)
                    if not last:
                        layernorm(g + 1, first + TX, k)
                copy_self(g, first, TX - 1)
            with act.Fori(XG, 2 * XG - 1) as g:
                second_lap(g, TX * (g - XG))
            second_lap(2 * XG - 1, NT - TX, last=True)

            def high_parts(e, b):
                for half, (a, z) in enumerate(HALVES):
                    act.wait_ge(raw_ld[half], 16 * (e + 1))
                    act.activation(w_hi[b][:, a:z], raw[:, a:z], ACT.Copy).then_inc(w_hi_ready, 1)
            def square(t, b, done):
                act.wait_ge(dev_ready, t + 1)
                act.activation(dev[:, b, 1], dev[:, b, 0], ACT.Square).then_inc(done, 1)

            def two_squares(i):
                stage(i, 0)
                square(2 * i - 2, 0, squared)
                stage(i, 1)
                square(2 * i - 1, 1, squared)
            two_squares(1)
            act.wait_ge(missed, 1)
            high_parts(0, 0)
            with act.Fori(2, NT // 2) as i:
                two_squares(i)
            stage(NT // 2, 0)
            square(NT - 3, 0, squared)
            square(NT - 2, 1, squared)
            square(NT - 1, 0, squared)
            act.wait_ge(flag_ready, 1)
            late = act.value_load(flag[0:1, 0:1], min_val=0, max_val=E)
            with act.If(late > 0):
                with act.Fori(0, NT) as t:
                    act.wait_ge(fx_dev, t + 1)
                    act.activation(dev[:, 0, 1], dev[:, 0, 0], ACT.Square).then_inc(fx_squared, 1)

            act.wait_ge(bn_scale, 1)
            act.activation(bnr[:, 1], bnr[:, 0], ACT.Sqrt, bias=eps[0:NP, 0:1]).then_inc(bnstd, 1)

            def copy_h2T(t):
                act.wait_ge(h2_turned, t + 1)
                if t >= TB:
                    act.wait_ge(logits_done, t - TB + 1)
                act.activation(hT[:, t % TB], PS[:, T_BANKS[t % TB], 0:KD * NP].rearrange("p (k n) -> p k n", k=KD),
                               ACT.Copy).then_inc(h2T_ready, 1)
            for g in range(XG):
                act.wait_ge(var2_ready, g + 1)
                act.activation(std[:, g * TX:(g + 1) * TX], mv[:, g * TX:(g + 1) * TX, 1], ACT.Sqrt,
                               bias=eps[0:NP, 0:1]).then_inc(std2_ready, 1)
                if g >= 1:
                    for t in range((g - 1) * TX, g * TX):
                        copy_h2T(t)
                act.wait_ge(nmr_ready, 2 + g + 1)
                for t in range(g * TX, (g + 1) * TX):
                    act.activation(Y[:, t, :], X[:, t, :], ACT.Identity, bias=nmr[:, t:t + 1],
                                   scale=rstd[:, t:t + 1]).then_inc(h2_ready, 1)
            for t in range((XG - 1) * TX, NT):
                copy_h2T(t)
            for n, (t0, t1) in enumerate(ROUTES):
                act.wait_ge(shifted, n + 1)
                act.activation(t8b[:, t0:t1], t8a[:, t0:t1], ACT.Exp).then_inc(exped, 1)

            act.wait_ge(b1_ready, 1)

            def high_rows(e):
                act.wait_ge(r_turned, e + 1)
                act.activation(buf_hi[:], PS[:, 0:KD, 0:SC], ACT.Copy).then_inc(buf_hi_ready, 1)

            def hidden(e):
                for f in range(KF):
                    act.wait_ge(hid_done, KF * e + f + 1)
                    act.wait_ge(hid_lo_ready, past(KF * e + f - 1) if f >= 2 else past(KF * e))
                    act.activation(hid[:, f % 2], PS[:, 2 + f % 2, 0:SC], ACT.Relu,
                                   bias=b1c[:, one(KF * e + f)]).then_inc(hid_relu, 1)
                    act.wait_ge(hid_relu, KF * e + f + 1)
                    act.wait_ge(ffn_done, past(e))
                    act.activation(hid_hi[:, f], hid[:, f % 2], ACT.Copy).then_inc(hid_hi_ready, 1)
            high_rows(0)
            act.wait_ge(scattered, 16 * NT)
            act.wait_ge(out_init, 16 * XG)
            hidden(0)
            high_parts(1, 1)
            high_rows(1)
            with act.Fori(1, NX // 2) as i:
                for b in range(2):
                    hidden(2 * i - 1 + b)
                    high_rows(2 * i + b)
                    high_parts(2 * i + b, b)
            hidden(NX - 1)

        @block.tensor
        def _(pe):
            for s in (h_turned, xw_done, ffn_done):
                pe.sem_inc(s, 1)
            pe.sem_inc(deg_counted, DPG)
            pe.wait_ge(ident_ready, 1)
            idn = ident[0:NP, 0:NP]

            def turn_edges(which):
                pe.wait_ge(erow_conv, which + 1)
                for k in range(NG):
                    mm = pe.transpose(PS[0:NP, which, k * GRP:(k + 1) * GRP], erow_f[:, which, k],
                                      ident[0:GRP, 0:GRP])
                mm.then_inc(erow_turned, 1)
            turn_edges(0)

            def turn_h(g, k):
                pe.wait_ge(h_ready, TX * g + k + 1)
                pe.wait_ge(hT_ready, past(free(g, k)))
                for c in range(KD):
                    mm = pe.transpose(PS[:, 3 + k % 2, c * NP:(c + 1) * NP], h5[:, k, c * 128:(c + 1) * 128], idn)
                mm.then_inc(h_turned, 1)

            def times_w(g, k, which):
                pe.wait_ge(hT_ready, past(TX * g + k + 1))
                pe.wait_ge(xw_copied, past(free(g, k)))
                for c in range(KD):
                    mm = pe.matmul(PS[0:NP, 5 + k % 2, 0:D], hT[:, k % 2, c], wcs[:, c, which * D:(which + 1) * D],
                                   start=(c == 0), stop=(c == KD - 1))
                mm.then_inc(xw_done, 1)

            def count(g, b):
                pe.wait_ge(onehot_deg, DPG * g + b + 1)
                for k in range(DC):
                    mm = pe.matmul(PS[0:NT, 2, 0:NP], onq[:, b, :, k], onr[:, b, :, k],
                                   start=False, stop=False, skip_group_check=True)
                mm.then_inc(deg_counted, 1)
            pe.wait_ge(consts, NCONST)
            pe.matmul(PS[0:NT, 2, 0:NP], ones[0:1, 0:NT], ones[0:1, :], start=True, stop=False, skip_group_check=True)
            turn_edges(1)
            pe.wait_ge(wcs_ld, 16 * 2 * KD)
            with pe.Fori(0, XG) as g:
                turn_h(g, 0)
                for k in range(TX):
                    if k + 1 < TX:
                        turn_h(g, k + 1)
                    times_w(g, k, 0)
                for b in range(DPG):
                    count(g, b)
            pe.wait_ge(b1_ld, 16)
            pe.transpose(PS[:, 7, 0:NX * KF], b1r[:], ident[0:NX * KF, 0:NX * KF]).then_inc(b1_turned, 1)
            pe.wait_ge(degsqrt, 1)
            pe.transpose(PS[0:NP, 0, 0:NT], sqdeg[:], ident[0:NT, 0:NT]).then_inc(degsqrt_turned, 1)
            with pe.Fori(XG, 2 * XG) as g:
                turn_h(g, 0)
                for k in range(TX):
                    if k + 1 < TX:
                        turn_h(g, k + 1)
                    times_w(g, k, 1)

            pe.wait_ge(b1_ready, 1)
            pe.wait_ge(dinv_ready, 1)

            def aggregate(t, par, start, skip, end, wraps):
                for b in range(NB):
                    pe.wait_ge(onehots, NB * t + b + 1)
                    for k in range(b * BATCH, (b + 1) * BATCH):
                        if k < skip or k >= end:
                            continue
                        c = start + k
                        pe.wait_ge(gathered[c % RING], 16 * (wraps + c // RING + 1))
                        if k == skip:
                            if not isinstance(t, int) or t >= 2:
                                pe.wait_ge(z_done, t - 1)
                        mm = pe.matmul(PS[0:NP, par, 0:D], OH[:, k], G[:, c % RING, :],
                                       start=(k == skip), stop=(k == end - 1))
                    mm.then_inc(batch_done, 1)

            def sum_dev(t, b, ready, stop=False):
                pe.wait_ge(ready, t + 1)
                for c in range(2):
                    mm = pe.matmul(PS[0:NP, 2 + c, 0:D], ones[:], dev[:, b, c], start=False, stop=stop,
                                   skip_group_check=True)
                return mm

            def zero_sums():
                for c in range(2):
                    pe.matmul(PS[0:NP, 2 + c, 0:D], nought[:], rows[:, 0], start=True, stop=False,
                              skip_group_check=True)
            half = CPT - MARGIN
            aggregate(0, 0, -MARGIN, MARGIN, WIN, 0)
            aggregate(1, 1, half, 0, WIN, 0)
            pe.wait_ge(z_done, 1)
            pe.matmul(PS[0:NP, 7, 0:D], ones[:], Z[:, 0, :], start=True, stop=True).then_inc(tile_summed, 1)
            zero_sums()

            def two_tiles(i):
                aggregate(2 * i, 0, -MARGIN, 0, WIN, i)
                sum_dev(2 * i - 2, 0, squared).then_inc(dev_summed, 1)
                aggregate(2 * i + 1, 1, half, 0, WIN, i)
                sum_dev(2 * i - 1, 1, squared).then_inc(dev_summed, 1)
            two_tiles(1)
            pe.wait_ge(missed, 1)
            pe.matmul(PS[0:1, 7, 0:1], ones[:, 0:1], missing[:], start=True, stop=True).then_inc(missed_sum, 1)
            with pe.Fori(2, NT // 2) as i:
                two_tiles(i)
            aggregate(NT - 1, 0, -MARGIN, 0, CPT + MARGIN, NT // 2)
            sum_dev(NT - 3, 0, squared).then_inc(dev_summed, 1)
            sum_dev(NT - 2, 1, squared).then_inc(dev_summed, 1)
            sum_dev(NT - 1, 0, squared, stop=True).then_inc(dev_summed, 1)

            pe.wait_ge(flag_ready, 1)
            late = pe.value_load(flag[0:1, 0:1], min_val=0, max_val=E)
            with pe.If(late > 0):
                with pe.Fori(0, NCH) as c:
                    with pe.Fori(0, NT) as t:
                        pe.wait_ge(fx_gathered, 16 * (c + 1))
                        pe.wait_ge(fx_onehot, NT * c + t + 1)
                        pe.matmul(PS[0:NP, 4, 0:D], OH[:, 0], G[:, 0, :], start=True, stop=True).then_inc(fx_mm, 1)
                zero_sums()
                with pe.Fori(0, NT) as t:
                    sum_dev(t, 0, fx_squared).then_inc(fx_summed, 1)

            pe.wait_ge(gate_ld, 32)

            def logits(t):
                pe.wait_ge(h2T_ready, t + 1)
                bank = L_BANKS[t >= ROUTES[1][0]]
                for k in range(KD):
                    mm = pe.matmul(PS[0:NP, bank, t * NX:(t + 1) * NX], hT[:, t % TB, k], wg[:, k],
                                   start=(k == 0), stop=(k == KD - 1))
                mm.then_inc(logits_done, 1)

            def count_tokens(n):
                t0, t1 = ROUTES[n]
                pe.wait_ge(picked, n + 1)
                pf = pick[:, t0:t1].rearrange("p t e -> p (t e)")
                a, z = t0 * NX, t1 * NX
                pe.matmul(PS[0:NP, 2, a:z], upper[:], pf, start=True, stop=True)
                pe.matmul(PS[0:NP, 3, a:z], ones[:], pf, start=True, stop=True).then_inc(counted, 1)
            for t in range(NT):
                pe.wait_ge(h2_ready, t + 1)
                if t >= TB:
                    pe.wait_ge(h2T_ready, t - TB + 1)
                for k in range(KD):
                    mm = pe.transpose(PS[:, T_BANKS[t % TB], k * NP:(k + 1) * NP], Y[:, t, k * 128:(k + 1) * 128], idn)
                mm.then_inc(h2_turned, 1)
                if t >= TB - 1:
                    logits(t - TB + 1)
                if t == NT - 1:
                    count_tokens(0)
            for t in range(NT - TB + 1, NT):
                logits(t)
            count_tokens(1)

            def turn_rows(e, i, b):
                pe.wait_ge(r_ld[b], 16 * (i + 1))
                for j in range(4):
                    for k in range(KD):
                        mm = pe.transpose(PS[:, k, j * SP4:(j + 1) * SP4], R[:, b, j, k * 128:(k + 1) * 128],
                                          ident[0:SP4, 0:SP4])
                mm.then_inc(r_turned, 1)

            def hidden(e, b):
                pe.wait_ge(buf_hi_ready, e + 1)
                pe.wait_ge(buf_lo_ready, e + 1)
                pe.wait_ge(w_hi_ready, 2 * e + 1)
                pe.wait_ge(w_lo_ready, 2 * e + 1)
                h, l = w1_of(w_hi[b]), w1_of(w_lo[b])
                for f in range(KF):
                    cols = slice(f * 128, (f + 1) * 128)
                    if f >= 2:
                        pe.wait_ge(hid_relu, KF * e + f - 1)
                    for k in range(KD):
                        pe.matmul(PS[:, 2 + f % 2, 0:SC], h[:, k, cols], buf_hi[:, k], start=(k == 0), stop=False)
                        pe.matmul(PS[:, 2 + f % 2, 0:SC], h[:, k, cols], buf_lo[:, k], start=False, stop=False)
                        mm = pe.matmul(PS[:, 2 + f % 2, 0:SC], l[:, k, cols], buf_hi[:, k],
                                       start=False, stop=(k == KD - 1))
                    mm.then_inc(hid_done, 1)

            def results(e, b):
                pe.wait_ge(w_hi_ready, 2 * e + 2)
                pe.wait_ge(w_lo_ready, 2 * e + 2)
                pe.wait_ge(y_copied, past(4 * e))
                h, l = w2_of(w_hi[b]), w2_of(w_lo[b])
                for f in range(KF):
                    pe.wait_ge(hid_lo_ready, past(KF * e + f + 1))
                    for j in range(4):
                        cols = slice(j * SP4, (j + 1) * SP4)
                        o = PS[0:SP4, 4 + j, 0:D]
                        pe.matmul(o, hid_hi[:, f, cols], h[:, f], start=(f == 0), stop=False)
                        pe.matmul(o, hid_hi[:, f, cols], l[:, f], start=False, stop=False)
                        mm = pe.matmul(o, hid_lo[:, f, cols], h[:, f], start=False, stop=(f == KF - 1))
                mm.then_inc(ffn_done, 1)
            turn_rows(0, 0, 0)
            hidden(0, 0)
            turn_rows(1, 0, 1)
            results(0, 0)
            with pe.Fori(1, NX // 2) as i:
                hidden(2 * i - 1, 1)
                turn_rows(2 * i, i, 0)
                results(2 * i - 1, 1)
                hidden(2 * i, 0)
                turn_rows(2 * i + 1, i, 1)
                results(2 * i, 0)
            hidden(NX - 1, 1)
            results(NX - 1, 1)

        @block.vector
        def _(dve):
            done = [0]

            def link(ins):
                done[0] += 1
                ins.then_inc(dve_step, 1)
                dve.wait_ge(dve_step, done[0])

            def flat(a):
                return a.rearrange("p a d -> p (a d)")

            for s in (y_copied, hid_lo_ready):
                dve.sem_inc(s, 1)
            dve.sem_inc(yb_free, 2)
            dve.wait_ge(dst_ld, 16)
            dve.tensor_copy(erow_f[:, 0], erow[:, 0]).then_inc(erow_conv, 1)

            def layer_stats(g, ready):
                for t in range(g * TX, (g + 1) * TX):
                    ins = dve.bn_stats(stats[:, t], X[:, t, :])
                link(ins)
                for t in range(g * TX, (g + 1) * TX):
                    ins = dve.bn_aggr(mv[:, t], stats[:, t])
                ins.then_inc(ready, 1)

            def layer_rstd(g, root):
                dve.wait_ge(root, g + 1)
                return dve.reciprocal(rstd[:, g * TX:(g + 1) * TX], std[:, g * TX:(g + 1) * TX])
            for g in range(XG):
                dve.wait_ge(x_ld[g], 16)
                layer_stats(g, var_ready)
                if g == 0:
                    dve.wait_ge(erow_turned, 1)
                    link(dve.tensor_copy(dstT[:], PS[0:NP, 0, 0:NCH]))
                    link(dve.tensor_scalar(qf[:], dstT[:], 1.0 / NP, 0.5 / NP - 0.5, ALU.mult, ALU.add))
                    link(dve.tensor_scalar(rf[:], qf[:], ROUND, None, ALU.add))
                    link(dve.tensor_scalar(qf[:], rf[:], ROUND, None, ALU.subtract))
                    dve.tensor_copy(q_bf[:], qf[:])
                    link(dve.scalar_tensor_tensor(out=r_bf[:], in0=qf[:], scalar=-float(NP), in1=dstT[:],
                                                  op0=ALU.mult, op1=ALU.add))
                if g == 1:
                    dve.wait_ge(src_ld, 16)
                    dve.tensor_copy(erow_f[:, 1], erow[:, 1]).then_inc(erow_conv, 1)
                if g >= 1:
                    layer_rstd(g - 1, std_ready).then_inc(rstd_ready, TX)
            layer_rstd(XG - 1, std_ready).then_inc(rstd_ready, TX)
            dve.wait_ge(lanes_ready, 1)
            dve.wait_ge(rstd_ready, NT)
            dve.scalar_tensor_tensor(out=nmr[:], in0=mv[:, :, 0], scalar=-1.0, in1=rstd[:], op0=ALU.mult,
                                     op1=ALU.mult).then_inc(nmr_ready, 1)
            dve.tensor_scalar(rstd1[:], rstd[:], 1.0, None, ALU.add).then_inc(nmr_ready, 1)

            def layernorm(g, first):
                dve.wait_ge(h_turned, past(TX * g))
                for k in range(TX):
                    dve.tensor_scalar(h5[:, k], flat(X[:, one(first + k), :]), mv[:, one(first + k), 0],
                                      rstd[:, one(first + k)], ALU.subtract, ALU.mult).then_inc(h_ready, 1)
            with dve.Fori(0, XG) as g:
                layernorm(g, TX * g)
                for b in range(DPG):
                    dve.wait_ge(deg_counted, DPG * g + b + 1)
                    c = bass.ds(DC * (DPG * g + b), DC)
                    dve.tensor_tensor(onq[:, b], q_bf[:, c].unsqueeze(1).to_broadcast([NP, NT, DC]), lanes[:, 0:NT],
                                      ALU.is_equal)
                    dve.tensor_tensor(onr[:, b], r_bf[:, c].unsqueeze(1).to_broadcast([NP, NP, DC]), lanes[:],
                                      ALU.is_equal).then_inc(onehot_deg, 1)

            dve.wait_ge(degsqrt_turned, 1)
            dve.reciprocal(dinv[:], PS[0:NP, 0, 0:NT]).then_inc(dinv_ready, 1)
            dve.wait_ge(dinv_ready, 1)
            dve.wait_ge(xw_copied, past(NT))
            for g in range(2):
                a, z = g * TX, (g + 1) * TX
                dve.tensor_tensor(Y[:, a:z, :], Y[:, a:z, :], dinv[:, a:z].unsqueeze(2).to_broadcast([NP, TX, D]),
                                  ALU.mult).then_inc(y_scaled[g], 1)

            def onehot_tile(t, par, skip, end, first=False):
                n = end - skip
                dve.tensor_scalar(dloc[:, par, skip:end], dstT[:, bass.ds(CPT * t - MARGIN + skip, n)],
                                  tile0[:, one(t)], None, ALU.subtract).then_inc(dloc_ready, 1)
                dve.wait_ge(dloc_ready, t + 1)
                for b in range(NB):
                    if not first:
                        dve.wait_ge(batch_done, NB * (t - 1) + b + 1)
                    for k in range(max(skip, b * BATCH), min(end, (b + 1) * BATCH)):
                        ins = dve.tensor_scalar(OH[:, k], lane[:], dloc[:, par, k:k + 1], None, ALU.is_equal)
                    ins.then_inc(onehots, 1)

            onehot_tile(0, 0, MARGIN, WIN, first=True)

            dve.wait_ge(nmr_ready, 2)
            dve.wait_ge(rows_ld, 64)
            link(dve.tensor_tensor(bnr[:, 0], rows[:, 0], rows[:, 1], ALU.add))
            with dve.Fori(XG, 2 * XG) as g:
                first = TX * (g - XG)
                dve.wait_ge(h_ready, TX * (g + 1))
                for k in range(TX):
                    t = one(first + k)
                    ins = dve.tensor_scalar(flat(X[:, t, :]), flat(X[:, t, :]), rstd1[:, t], nmr[:, t],
                                            ALU.mult, ALU.add)
                ins.then_inc(xh_ready, 1)
                dve.wait_ge(xw_copied, past(TX * (g + 1)))
                piece = Z[:, bass.ds(first, TX), :]
                dve.tensor_tensor(piece, piece, bnr[:, 0].unsqueeze(1).to_broadcast([NP, TX, D]), ALU.add) \
                   .then_inc(z_biased, 1)
            for g in range(XG):
                dve.wait_ge(y_scaled[g], TX if g in (2, 3) else 1)
            dve.wait_ge(z_biased, XG)

            def own_messages(t):
                dve.scalar_tensor_tensor(out=flat(Z[:, one(t), :]), in0=flat(Y[:, one(t), :]), scalar=dinv[:, one(t)],
                                         in1=flat(Z[:, one(t), :]), op0=ALU.mult, op1=ALU.add).then_inc(own_added, 1)

            def finish_tile(t, par):
                dve.wait_ge(own_added, t + 1)
                dve.wait_ge(batch_done, NB * (t + 1))
                dve.scalar_tensor_tensor(out=flat(Z[:, one(t), :]), in0=PS[0:NP, par, 0:D], scalar=dinv[:, one(t)],
                                         in1=flat(Z[:, one(t), :]), op0=ALU.mult, op1=ALU.add).then_inc(z_done, 1)
            def deviate(t, b, first=False):
                if not first:
                    dve.wait_ge(dev_summed, t - 1)
                dve.tensor_tensor(dev[:, b, 0], flat(Z[:, one(t), :]), shift[:], ALU.subtract).then_inc(dev_ready, 1)
            dve.memset(nought[:], 0.0)
            link(dve.memset(XY[:, :, D:RES], 0.0))
            link(dve.tensor_copy(XY[:, :, TOK], tokid[:]))
            own_messages(0)
            onehot_tile(1, 1, 0, WIN)
            own_messages(1)
            finish_tile(0, 0)
            onehot_tile(2, 0, 0, WIN)
            own_messages(2)
            finish_tile(1, 1)
            dve.wait_ge(tile_summed, 1)
            link(dve.tensor_scalar(shift[:], PS[0:NP, 7, 0:D], 1.0 / NP, None, ALU.mult))
            dve.wait_ge(z_done, 2)
            deviate(0, 0, True)
            deviate(1, 1, True)
            onehot_tile(3, 1, 0, WIN)
            own_messages(3)
            finish_tile(2, 0)

            link(dve.tensor_tensor(rf[:], dstT[:], lo[:], ALU.is_lt))
            link(dve.tensor_tensor(qf[:], dstT[:], hi[:], ALU.is_ge))
            link(dve.tensor_tensor(rf[:], rf[:], qf[:], ALU.add))
            dve.reduce_sum(missing[:], rf[:], axis=AX_X).then_inc(missed, 1)
            link(dve.scalar_tensor_tensor(out=qf[:], in0=dstT[:], scalar=1.0, in1=rf[:], op0=ALU.add, op1=ALU.mult))
            link(dve.tensor_scalar(qf[:], qf[:], -1.0, None, ALU.add))
            dve.wait_ge(missed_sum, 1)
            dve.tensor_copy(flag[:], PS[0:1, 7, 0:1]).then_inc(flag_ready, 1)

            for half, (a, z) in enumerate(HALVES):
                dve.wait_ge(w_hi_ready, half + 1)
                dve.tensor_tensor(w_lo[0][:, a:z], raw[:, a:z], w_hi[0][:, a:z].bitcast(F32),
                                  ALU.subtract).then_inc(w_lo_ready, 1)

            with dve.Fori(2, NT // 2) as i:
                for b in range(2):
                    t = 2 * i + b
                    onehot_tile(t, b, 0, WIN)
                    own_messages(t)
                    finish_tile(t - 1, 1 - b)
                    dve.wait_ge(z_done, t - 1)
                    deviate(t - 2, b)
            onehot_tile(NT - 1, 0, 0, CPT + MARGIN)
            own_messages(NT - 1)
            finish_tile(NT - 2, 1)
            dve.wait_ge(z_done, NT - 1)
            deviate(NT - 3, 0)
            deviate(NT - 2, 1)
            finish_tile(NT - 1, 0)
            dve.wait_ge(z_done, NT)
            deviate(NT - 1, 0)

            late = dve.value_load(flag[0:1, 0:1], min_val=0, max_val=E)
            with dve.If(late > 0):
                with dve.Fori(0, NCH) as c:
                    dve.tensor_scalar(fx_loc[:], tile0[:], -1.0, qf[:, one(c)], ALU.mult, ALU.add) \
                       .then_inc(fx_located, 1)
                    dve.tensor_copy(fx_idx[:], srcT[:, one(c)]).then_inc(fx_staged, 1)
                    with dve.Fori(0, NT) as t:
                        dve.wait_ge(fx_located, c + 1)
                        dve.tensor_scalar(OH[:, 0], lane[:], fx_loc[:, one(t)], None, ALU.is_equal) \
                           .then_inc(fx_onehot, 1)
                        dve.wait_ge(fx_mm, NT * c + t + 1)
                        dve.scalar_tensor_tensor(out=flat(Z[:, one(t), :]), in0=PS[0:NP, 4, 0:D],
                                                 scalar=dinv[:, one(t)], in1=flat(Z[:, one(t), :]),
                                                 op0=ALU.mult, op1=ALU.add).then_inc(fx_added, 1)
                        dve.wait_ge(fx_added, NT * c + t + 1)
                dve.wait_ge(dev_summed, NT)
                with dve.Fori(0, NT) as t:
                    dve.tensor_tensor(dev[:, 0, 0], flat(Z[:, one(t), :]), shift[:], ALU.subtract).then_inc(fx_dev, 1)
                    hold(dve, fx_summed, t + 1)

            dve.wait_ge(dev_summed, NT)
            link(dve.tensor_scalar(bnr[:, 3], PS[0:NP, 2, 0:D], 1.0 / N, None, ALU.mult))
            dve.tensor_tensor(shift[:], shift[:], bnr[:, 3], ALU.add)
            link(dve.tensor_tensor(bnr[:, 2], bnr[:, 3], bnr[:, 3], ALU.mult))
            dve.scalar_tensor_tensor(out=bnr[:, 0], in0=PS[0:NP, 3, 0:D], scalar=1.0 / N, in1=bnr[:, 2],
                                     op0=ALU.mult, op1=ALU.subtract).then_inc(bn_scale, 1)
            dve.wait_ge(bnstd, 1)
            link(dve.reciprocal(bnr[:, 2], bnr[:, 1]))
            link(dve.tensor_tensor(bnr[:, 2], bnr[:, 2], rows[:, 2], ALU.mult))
            link(dve.tensor_tensor(bnr[:, 3], shift[:], bnr[:, 2], ALU.mult))
            dve.tensor_tensor(bnr[:, 3], rows[:, 3], bnr[:, 3], ALU.subtract).then_inc(bn_rows, 1)
            dve.wait_ge(bn_rows, 1)

            def layer_norms(g):
                link(layer_rstd(g, std2_ready))
                a, z = g * TX, (g + 1) * TX
                dve.scalar_tensor_tensor(out=nmr[:, a:z], in0=mv[:, a:z, 0], scalar=-1.0, in1=rstd[:, a:z],
                                         op0=ALU.mult, op1=ALU.mult).then_inc(nmr_ready, 1)
            for g in range(XG):
                a, z = g * TX, (g + 1) * TX
                piece = Z[:, a:z, :]
                if g in BN_POOL:
                    dve.wait_ge(bn_part, g - BN_POOL[0] + 1)
                else:
                    link(dve.tensor_tensor(piece, piece, bnr[:, 2].unsqueeze(1).to_broadcast([NP, TX, D]), ALU.mult))
                    link(dve.tensor_tensor(piece, piece, bnr[:, 3].unsqueeze(1).to_broadcast([NP, TX, D]), ALU.add))
                dve.scalar_tensor_tensor(out=X[:, a:z, :], in0=piece, scalar=0.0, in1=X[:, a:z, :],
                                         op0=ALU.max, op1=ALU.add).then_inc(x2_ready, 1)
                dve.wait_ge(x2_ready, g + 1)
                layer_stats(g, var2_ready)
                if g >= 1:
                    layer_norms(g - 1)
            layer_norms(XG - 1)

            before = PS[0:NP, 2, 0:NT * NX].rearrange("p (t e) -> p t e", e=NX)
            whole = PS[0:NP, 3, 0:NT * NX].rearrange("p (t e) -> p t e", e=NX)
            dve.memset(carry[:], 0.0)

            def route(n):
                t0, t1 = ROUTES[n]
                nt = t1 - t0
                best, total, prob, chosen, place, kept = (v25[:, c, t0:t1] for c in range(6))

                def wide(a):
                    return a.unsqueeze(2).to_broadcast([NP, nt, NX])
                logit = PS[0:NP, L_BANKS[n], 0:NT * NX].rearrange("p (t e) -> p t e", e=NX)
                L, P8, A8, B8 = lg[:, t0:t1], pick[:, t0:t1], t8a[:, t0:t1], t8b[:, t0:t1]
                dve.wait_ge(logits_done, t1)
                link(dve.tensor_tensor(L, logit[:, t0:t1], gbrow[:].unsqueeze(1).to_broadcast([NP, nt, NX]), ALU.add))
                link(dve.tensor_reduce(best, L, AX_X, ALU.max))
                dve.tensor_tensor(A8, L, wide(best), ALU.subtract).then_inc(shifted, 1)
                link(dve.tensor_tensor(P8, L, wide(best), ALU.is_equal))
                link(dve.tensor_scalar(L, xid[:, t0:t1], -1.0, float(NX), ALU.mult, ALU.add))
                link(dve.tensor_tensor(L, L, P8, ALU.mult))
                link(dve.tensor_reduce(chosen, L, AX_X, ALU.max))
                dve.tensor_tensor(P8, L, wide(chosen), ALU.is_equal).then_inc(picked, 1)
                dve.wait_ge(picked, n + 1)
                dve.wait_ge(exped, n + 1)
                link(dve.tensor_reduce(total, B8, AX_X, ALU.add))
                link(dve.reciprocal(prob, total))
                link(dve.tensor_copy(XY[:, t0:t1, PRB], prob))

                dve.wait_ge(counted, n + 1)
                dve.tensor_copy(A8[:, 0], carry[:])
                link(dve.tensor_copy(A8[:, 1:nt], whole[:, t0:t1 - 1]))
                now, then = A8, B8
                step = 1
                while step < nt:
                    dve.tensor_copy(then[:, 0:step], now[:, 0:step])
                    link(dve.tensor_tensor(then[:, step:nt], now[:, step:nt], now[:, 0:nt - step], ALU.add))
                    now, then = then, now
                    step *= 2
                dve.tensor_tensor(carry[:], now[:, nt - 1], whole[:, t1 - 1], ALU.add)
                link(dve.tensor_tensor(then, now, before[:, t0:t1], ALU.add))
                link(dve.tensor_tensor(then, then, P8, ALU.mult))
                link(dve.tensor_reduce(place, then, AX_X, ALU.add))
                link(dve.tensor_scalar(kept, place, float(CAP), None, ALU.is_le))
                link(dve.tensor_scalar(kept, kept, -NOWHERE, NOWHERE, ALU.mult, ALU.add))
                link(dve.scalar_tensor_tensor(out=place, in0=chosen, scalar=-float(SLOTS), in1=place,
                                              op0=ALU.mult, op1=ALU.add))
                link(dve.tensor_scalar(place, place, float(NX * SLOTS - 1), None, ALU.add))
                dve.tensor_tensor(slot_i[:, t0:t1], place, kept, ALU.add).then_inc(slots_ready, 1)
            for n in range(len(ROUTES)):
                route(n)

            def low_rows(e):
                dve.wait_ge(buf_hi_ready, e + 1)
                dve.tensor_tensor(buf_lo[:], PS[:, 0:KD, 0:SC], buf_hi[:].bitcast(F32),
                                  ALU.subtract).then_inc(buf_lo_ready, 1)

            def low_hidden(e):
                for f in range(KF):
                    dve.wait_ge(hid_hi_ready, KF * e + f + 1)
                    dve.tensor_tensor(hid_lo[:, f], hid[:, f % 2], hid_hi[:, f].bitcast(F32),
                                      ALU.subtract).then_inc(hid_lo_ready, 1)
            base, LINKS = done[0], 7

            def take_results(e, b):
                dve.wait_ge(ffn_done, past(e + 1))
                dve.wait_ge(yb_free, e + 1)
                for j in range(4):
                    dve.tensor_tensor(yb[:, b, j], PS[0:SP4, 4 + j, 0:D], flat(b2row[:, one(e), :]),
                                      ALU.add).then_inc(y_copied, 1)

            def finish(e, i, b):
                n = 0

                def then(ins):
                    nonlocal n
                    n += 1
                    ins.then_inc(dve_step, 1)
                    hold(dve, dve_step, LINKS * e + (base + n))
                hold(dve, tail_ld[b], 16 * (i + 1))
                dve.tensor_copy(tok_i[:, b], tail[:, b, :, TOK - D])
                dve.wait_ge(y_copied, past(4 * e + 4))
                for j in range(4):
                    ins = dve.tensor_scalar(yb[:, b, j], yb[:, b, j], tail[:, b, j, PRB - D:PRB - D + 1], None,
                                            ALU.mult)
                then(ins)
                y = yb[:, b].rearrange("p j d -> p (j d)")
                then(dve.tensor_scalar(fin_a[:], y, FLT_MAX, None, ALU.is_le))
                then(dve.scalar_tensor_tensor(out=fin_b[:], in0=y, scalar=-FLT_MAX, in1=fin_a[:],
                                              op0=ALU.is_ge, op1=ALU.subtract))
                then(dve.tensor_scalar(fin_b[:], fin_b[:], INFINITE, None, ALU.mult))
                then(dve.scalar_tensor_tensor(out=fin_a[:].bitcast(I32), in0=y, scalar=-FLT_MAX, in1=fin_a[:],
                                              op0=ALU.is_ge, op1=ALU.mult))
                then(dve.copy_predicated(fin_b[:], fin_a[:].bitcast(I32), y))
                then(dve.tensor_tensor(yb[:, b], fin_b[:].rearrange("p (j d) -> p j d", j=4),
                                       tail[:, b, :, RES - D:ROW - D], ALU.add))
                dve.sem_inc(y_ready, 1)
                assert n == LINKS
            low_rows(0)
            low_hidden(0)
            low_rows(1)
            dve.wait_ge(b2_ld, 16)
            with dve.Fori(1, NX // 2) as i:
                take_results(2 * i - 2, 0)
                low_hidden(2 * i - 1)
                low_rows(2 * i)
                finish(2 * i - 2, i - 1, 0)
                take_results(2 * i - 1, 1)
                low_hidden(2 * i)
                low_rows(2 * i + 1)
                finish(2 * i - 1, i - 1, 1)
            take_results(NX - 2, 0)
            low_hidden(NX - 1)
            finish(NX - 2, NX // 2 - 1, 0)
            take_results(NX - 1, 1)
            finish(NX - 1, NX // 2 - 1, 1)


INPUTS = ["x", "src", "dst", "L0_gnn_conv_weight", "L0_gnn_conv_bias", "L0_gnn_self_weight", "L0_gnn_bias",
          "L0_gnn_gamma", "L0_gnn_beta", "L0_ffn_gate_w", "L0_ffn_gate_b", "L0_ffn_w1", "L0_ffn_b1",
          "L0_ffn_w2", "L0_ffn_b2"]


def kernel(**inputs):
    import numpy as np
    import concourse.bacc as bacc
    from concourse.bass_utils import run_bass_kernel_spmd

    nc = bacc.Bacc("TRN2", target_bir_lowering=False, num_devices=1)
    arrays, args = {}, []
    for name in INPUTS:
        a = np.ascontiguousarray(inputs[name])
        arrays[f"in_{name}"] = a
        args.append(nc.dram_tensor(f"in_{name}", a.shape, mybir.dt.from_np(a.dtype), kind="ExternalInput").ap())
    shape = arrays["in_x"].shape
    args.append(nc.dram_tensor("out", shape, F32, kind="ExternalOutput").ap())
    gnn_then_moe(nc, *args)
    r = run_bass_kernel_spmd(nc, [arrays], core_ids=[0])
    return r.results[0]["out"]
```

```python
from contextlib import ExitStack
from math import ceil

import concourse.bass as bass
from concourse import mybir

ALU = mybir.AluOpType
ACT = mybir.ActivationFunctionType
AX_X = mybir.AxisListType.X
F32 = mybir.dt.float32
F32R = mybir.dt.float32r
BF16 = mybir.dt.bfloat16
I32 = mybir.dt.int32

NT = 25
MARGIN = 4
BATCH = 8
CG = 4
DPG = 4
DB = 2
TB = 3
XG = 5
EPS = 1e-5
ROUND = 12582912.0
NOWHERE = 1.0e6
FLT_MAX = 3.4028234663852886e38
CAPACITY_FACTOR = 1.25
INFINITE = 1.0e4
LG = 4
CREDIT = 3
BUFFER = (0, 1, 0, 1, 2)
H_BANKS = (3, 4, 1)
W_BANKS = (5, 6, 7)
T_BANKS = (5, 6, 7)
E_BANKS = (4, 1)
L_BANKS = (2, 3, 2)
COUNTS = {14: 0, 20: 1}
EXPS = {15: 0, 21: 1}


def gnn_then_moe(nc, x, src, dst, conv_w, conv_b, self_w, self_b, gamma, beta,
                 gate_w, gate_b, w1, b1, w2, b2, out):
    N, D = x.shape
    E = src.shape[0]
    NX, _, F = w1.shape
    NP = N // NT
    NCH = E // NP
    CPT = NCH // NT
    WIN = CPT + 2 * MARGIN
    RING = 2 * CPT
    NB = WIN // BATCH
    KD = D // 128
    KF = F // 128
    CAP = max(1, ceil(CAPACITY_FACTOR * N / NX))
    SLOTS = 512
    SP4 = ceil(CAP / 4)
    SC = 4 * SP4
    TOK, PRB, RES = D, D + 1, D + 4
    ROW = RES + D
    GRP = 100
    NG = NCH // GRP
    HALVES = ((0, KD * F), (KD * F, KD * F + KF * D))
    BN_POOL = (1, 2, 3)
    ROUTES = ((0, 2 * LG), (2 * LG, 4 * LG), (4 * LG, NT))
    NQ = ceil(NT / LG)
    TX = NT // XG
    DC = NCH // (CG * DPG)
    NDEG = CG * DPG

    def owner(t):
        if t // TX == XG - 1:
            return "dve"
        return "pool" if t // TX >= 1 and t % TX >= 2 else "act"

    def h2_count(who, tiles):
        return sum(owner(t) == who for t in range(tiles))

    assert NT * NP == N and NCH * NP == E and CPT * NT == NCH and SC <= SLOTS
    assert WIN % BATCH == 0 and MARGIN * 2 == BATCH and NT % 2 == 1 and NX % 2 == 0

    table = nc.dram_tensor("message_table", (N, D), F32).ap()
    slots = nc.dram_tensor("dispatched_rows", (NX * SLOTS, ROW), F32).ap()

    with ExitStack() as ctx:
        def sb(name, shape, dt=F32):
            return ctx.enter_context(nc.sbuf_tensor(name, shape, dt))

        def sem(name):
            return ctx.enter_context(nc.semaphore(name))

        FB = 4
        MATRICES = (KD * F + KF * D) * FB
        SIZES = (52 * 1024, NT * D * FB, RING * D * FB, 12 * 1024, 2 * MATRICES, MATRICES)
        arena_at = ceil(nc.sbuf_base / 32) * 32
        sb("arena", [128, sum(SIZES) // FB])

        class Part:

            def __init__(self, start, size):
                self.at, self.end = arena_at + start, arena_at + start + size

            def place(self, name, shape, dt=F32):
                size = 2 if dt == BF16 else 4
                for n in shape[1:]:
                    size *= n
                t = nc.alloc_sbuf_tensor_at(name, shape, dt, offset=self.at)
                self.at += ceil(size / 32) * 32
                assert self.at <= self.end, name
                return t

        def part(n):
            return Part(sum(SIZES[:n]), SIZES[n])

        XY = part(0).place("XY", [NP, NT, ROW])
        Y = XY[:, :, 0:D]
        X = XY[:, :, RES:ROW]
        Z = part(1).place("Z", [NP, NT, D])
        G = part(2).place("G", [NP, RING, D])
        OH = part(3).place("OH", [NP, WIN, NP])
        p = part(2)
        onr = p.place("onr", [NP, DB, NP, DC], BF16)
        onq = p.place("onq", [NP, DB, NT, DC], BF16)
        p = part(4)
        wcs = p.place("wcs", [128, KD, 2 * D])
        lanes = p.place("lanes", [NP, NP, DC], BF16)
        erow = p.place("erow", [GRP, 2, NG, NP], I32)
        erow_f = p.place("erow_f", [GRP, 2, NG, NP])
        h5 = p.place("h5", [NP, TX, D])
        lo = p.place("lo", [NP, NCH])
        hi = p.place("hi", [NP, NCH])
        p = part(2)
        lgT = p.place("lgT", [NX, 2, LG * NP])
        t8a = p.place("t8a", [NP, NT, NX])
        t8b = p.place("t8b", [NP, NT, NX])
        raw = part(5).place("raw", [128, KD * F + KF * D])
        w_hi, w_lo = [], []
        for b, p in enumerate((part(4), part(0))):
            w_hi.append(p.place(f"w_hi{b}", [128, KD * F + KF * D], F32R))
            w_lo.append(p.place(f"w_lo{b}", [128, KD * F + KF * D], F32R))
        b2row = p.place("b2row", [SP4, NX, D])
        hid = p.place("hid", [128, 2, SC])
        fin_a = p.place("fin_a", [SP4, 4 * D])
        p = part(1)
        R = p.place("R", [SP4, 2, 4, D])
        tail = p.place("tail", [SP4, 2, 4, ROW - D])
        yb = p.place("yb", [SP4, 2, 4, D])
        p = part(2)
        hid_hi = p.place("hid_hi", [128, KF, SC], F32R)
        hid_lo = p.place("hid_lo", [128, KF, SC], F32R)
        p = part(3)
        buf_hi = p.place("buf_hi", [128, KD, SC], F32R)
        buf_lo = p.place("buf_lo", [128, KD, SC], F32R)
        fin_b = p.place("fin_b", [SP4, 4 * D])

        def w1_of(a):
            return a[:, 0:KD * F].rearrange("p (k f) -> p k f", k=KD)

        def w2_of(a):
            return a[:, KD * F:].rearrange("p (k d) -> p k d", k=KF)

        empty = sb("empty", [SP4, 1, ROW])
        ident = sb("ident", [128, 128])
        ones = sb("ones", [NP, NP])
        ones_bf = sb("ones_bf", [NP, NP], BF16)
        upper = sb("upper", [NP, NP], BF16)
        lane = sb("lane", [NP, NP])
        tile0 = sb("tile0", [NP, NT])
        tokid = sb("tokid", [NP, NT])
        rank = sb("rank", [NP, NT, NX])
        eps = sb("eps", [128, 1])
        wg = sb("wg", [128, KD, NX])
        rows = sb("rows", [NP, 4, D])
        gb = sb("gb", [NX, 1])
        b1r = sb("b1r", [NX * KF, 128])
        b1c = sb("b1c", [128, NX * KF])
        dstT = sb("dstT", [NP, NCH])
        srcT = sb("srcT", [NP, NCH], I32)
        qf = sb("qf", [NP, NCH])
        rf = sb("rf", [NP, NCH])
        q_bf = sb("q_bf", [NP, NCH], BF16)
        r_bf = sb("r_bf", [NP, NCH], BF16)
        missing = sb("missing", [NP, 1])
        flag = sb("flag", [1, 1], I32)
        idx = sb("idx", [NP, RING], I32)
        dloc = sb("dloc", [NP, 2, WIN])
        stats = sb("stats", [NP, NT, 6])
        mv = sb("mv", [NP, NT, 2])
        std = sb("std", [NP, NT])
        rstd = sb("rstd", [NP, NT])
        nmr = sb("nmr", [NP, NT])
        rstd1 = sb("rstd1", [NP, NT])
        sqdeg = sb("sqdeg", [NT, NP])
        dinv = sb("dinv", [NP, NT])
        hT = sb("hT", [128, TB, KD, NP])
        dev = sb("dev", [NP, 2, 2, D])
        fx_idx = sb("fx_idx", [NP, 1], I32)
        fx_loc = sb("fx_loc", [NP, NT])
        nought = sb("nought", [NP, NP])
        shift = sb("shift", [NP, D])
        bnr = sb("bnr", [NP, 4, D])
        lg = sb("lg", [NP, NT, NX])
        pick = sb("pick", [NP, NT, NX], BF16)
        v25 = sb("v25", [NP, 5, NT])
        slot_i = sb("slot_i", [NP, NT], I32)
        tok_i = sb("tok_i", [SP4, 2, 4], I32)

        PS = ctx.enter_context(nc.psum_tensor("PS", [128, 8, 512], F32))

        dst_ld, src_ld = sem("dst_ld"), sem("src_ld")
        z_biased, own_added = sem("z_biased"), sem("own_added")
        x_ld = [sem(f"x_ld{g}") for g in range(XG)]
        wcs_ld, rows_ld, gate_ld, b1_ld, b2_ld = (sem(s) for s in ("wcs_ld", "rows_ld", "gate_ld", "b1_ld", "b2_ld"))
        consts, ident_ready, lanes_ready = sem("consts"), sem("ident_ready"), sem("lanes_ready")
        passed = sem("passed")
        pool_step = sem("pool_step")
        dve_step = sem("dve_step")
        erow_conv = sem("erow_conv")
        erow_turned = sem("erow_turned")
        src_ready = sem("src_ready")
        b1_turned, b1_ready = sem("b1_turned"), sem("b1_ready")
        empties_stored = sem("empties_stored")
        var_ready, std_ready, rstd_ready = sem("var_ready"), sem("std_ready"), sem("rstd_ready")
        h_ready, xh_ready, h_turned, hT_ready, xw_done, xw_copied = (
            sem(s) for s in ("h_ready", "xh_ready", "h_turned", "hT_ready", "xw_done", "xw_copied"))
        onehot_deg, deg_counted, degsqrt, degsqrt_turned, dinv_ready = (
            sem(s) for s in ("onehot_deg", "deg_counted", "degsqrt", "degsqrt_turned", "dinv_ready"))
        y_scaled = [sem(f"y_scaled{g}") for g in range(CG)]
        table_stored = sem("table_stored")
        idx_staged = sem("idx_staged")
        gathered = [sem(f"gathered{s}") for s in range(RING)]
        missed, missed_sum, flag_ready = sem("missed"), sem("missed_sum"), sem("flag_ready")
        dloc_ready, onehots, batch_done, z_done = (
            sem(s) for s in ("dloc_ready", "onehots", "batch_done", "z_done"))
        fx_staged, fx_gathered, fx_onehot, fx_mm, fx_added = (
            sem(s) for s in ("fx_staged", "fx_gathered", "fx_onehot", "fx_mm", "fx_added"))
        fx_located, fx_dev, fx_squared, fx_summed = (
            sem(s) for s in ("fx_located", "fx_dev", "fx_squared", "fx_summed"))
        tile_summed, dev_ready, squared, dev_summed, bn_scale, bnstd, bn_rows, bn_part, x2_ready = (
            sem(s) for s in ("tile_summed", "dev_ready", "squared", "dev_summed", "bn_scale", "bnstd",
                             "bn_rows", "bn_part", "x2_ready"))
        out_init = sem("out_init")
        var2_ready, std2_ready, nmr_ready, h2_turned, h2T_ready = (
            sem(s) for s in ("var2_ready", "std2_ready", "nmr_ready", "h2_turned", "h2T_ready"))
        h2_ready = {who: sem(f"h2_ready_{who}") for who in ("act", "pool", "dve")}
        logits_done, logits_copied, logits_turned = (
            sem(s) for s in ("logits_done", "logits_copied", "logits_turned"))
        shifted, exped, picked, counted, slots_ready, probs_ready, scattered = (
            sem(s) for s in ("shifted", "exped", "picked", "counted", "slots_ready", "probs_ready", "scattered"))
        raw_ld = [sem(f"raw_ld{half}") for half in range(2)]
        w_hi_ready, w_lo_ready = sem("w_hi_ready"), sem("w_lo_ready")
        r_ld = [sem(f"r_ld{b}") for b in range(2)]
        tail_ld = [sem(f"tail_ld{b}") for b in range(2)]
        r_turned, buf_hi_ready, buf_lo_ready, hid_done, hid_relu, hid_hi_ready, hid_lo_ready = (
            sem(s) for s in ("r_turned", "buf_hi_ready", "buf_lo_ready", "hid_done", "hid_relu", "hid_hi_ready",
                             "hid_lo_ready"))
        ffn_done, y_copied, y_ready, yb_free = (sem(s) for s in ("ffn_done", "y_copied", "y_ready", "yb_free"))
        placed = [sem(f"placed{b}") for b in range(2)]

        NCONST = 10

        block = ctx.enter_context(nc.Block())

        def one(n):
            return bass.ds(n, 1)

        def hold(eng, s, n):
            eng.wait_ge(s, n)
            eng.sem_inc(passed, 1)

        def past(n):
            return n + CREDIT

        def free(g, k):
            earlier = [n for n in range(-TX, k) if BUFFER[n % TX] == BUFFER[k]]
            return TX * g + earlier[-1] + 1

        @block.sync
        def _(sp):
            def edge_list(a):
                return a.rearrange("(k p j) -> p k j", k=NG, j=NP)

            sp.dma_start(erow[:, 0], edge_list(dst)).then_inc(dst_ld, 16)
            xt = x.rearrange("(t p) d -> p t d", p=NP)
            for g in range(XG):
                sp.dma_start(X[:, g * TX:(g + 1) * TX, :], xt[:, g * TX:(g + 1) * TX, :]).then_inc(x_ld[g], 16)
                if g == 0:
                    sp.dma_start(erow[:, 1], edge_list(src)).then_inc(src_ld, 16)

            def weights(e, first=False):
                sources = (w1[one(e)].rearrange("a (k p) f -> p (a k) f", p=128),
                           w2[one(e)].rearrange("a (k p) d -> p (a k) d", p=128))
                for half, (place, source) in enumerate(zip((w1_of(raw), w2_of(raw)), sources)):
                    if not first:
                        sp.wait_ge(w_hi_ready, 2 * e - 1 + half)
                        sp.wait_ge(w_lo_ready, 2 * e - 1 + half)
                    sp.dma_start(place, source).then_inc(raw_ld[half], 16)

            def load_rows(e, b):
                sp.dma_start(R[:, b], slots[bass.ds(e * SLOTS, SC), 0:D]
                             .rearrange("(p j) c -> p j c", j=4)).then_inc(r_ld[b], 16)

            def load_tail(e, b):
                sp.dma_start(tail[:, b], slots[bass.ds(e * SLOTS, SC), D:ROW]
                             .rearrange("(p j) c -> p j c", j=4)).then_inc(tail_ld[b], 16)

            weights(0, True)
            sp.wait_ge(consts, NCONST)
            for e in range(NX):
                sp.dma_start(slots[e * SLOTS:e * SLOTS + SC, :].rearrange("(p j) c -> p j c", j=4),
                             empty[:].to_broadcast([SP4, 4, ROW])).then_inc(empties_stored, 16)
            tt = table.rearrange("(t p) d -> p t d", p=NP)
            for g in range(XG):
                if g < CG:
                    sp.wait_ge(y_scaled[g], 1)
                else:
                    sp.wait_ge(xw_copied, past(TX * (g + 1)))
                sp.dma_start(tt[:, g * TX:(g + 1) * TX, :],
                             Y[:, g * TX:(g + 1) * TX, :]).then_inc(table_stored, 16)
            weights(1)
            ot = out.rearrange("(t p) d -> p t d", p=NP)
            for g in range(XG):
                sp.wait_ge(x2_ready, g + 1)
                sp.dma_start(ot[:, g * TX:(g + 1) * TX, :], X[:, g * TX:(g + 1) * TX, :]).then_inc(out_init, 16)
            sp.wait_ge(scattered, 16 * NT)
            for b in range(2):
                load_rows(b, b)
            for b in range(2):
                load_tail(b, b)
            sp.wait_ge(out_init, 16 * XG)
            sp.dma_start(b2row[:], b2.rearrange("(a e) d -> a e d", a=1).to_broadcast([SP4, NX, D])).then_inc(b2_ld, 16)

            def inputs(e, b):
                sp.wait_ge(r_turned, e - 1)
                load_rows(e, b)
                weights(e)

            def tokens(e, i, b):
                sp.wait_ge(y_ready, e - 1)
                load_tail(e, b)
                sp.wait_ge(placed[b], 64 * i)
                sp.sem_inc(yb_free, 1)
            inputs(2, 0)
            with sp.Fori(1, NX // 2 - 1) as i:
                inputs(2 * i + 1, 1)
                tokens(2 * i, i, 0)
                inputs(2 * i + 2, 0)
                tokens(2 * i + 1, i, 1)
            inputs(NX - 1, 1)
            for b in range(2):
                tokens(NX - 2 + b, NX // 2 - 1, b)
            for b in range(2):
                sp.wait_ge(placed[b], 16 * 4 * (NX // 2))

        @block.gpsimd
        def _(pool):
            pool.memset(ident[:], 0.0).then_inc(pool_step, 1)
            pool.memset(upper[:], 1.0).then_inc(pool_step, 1)
            pool.memset(ones[:], 1.0).then_inc(consts, 1)
            pool.memset(ones_bf[:], 1.0).then_inc(consts, 1)
            pool.memset(eps[:], EPS).then_inc(consts, 1)
            pool.wait_ge(pool_step, 2)
            pool.affine_select(out=ident[:], in_=ident[:], compare_op=ALU.not_equal, fill=1.0, base=0,
                               pattern=[[-1, 128]], channel_multiplier=1).then_inc(ident_ready, 1)
            pool.affine_select(out=upper[:], in_=upper[:], compare_op=ALU.is_ge, fill=0.0, base=0,
                               pattern=[[1, NP]], channel_multiplier=-1).then_inc(consts, 1)
            pool.iota(lanes[:], [[1, NP], [0, DC]], base=0, channel_multiplier=0,
                      allow_small_or_imprecise_dtypes=True).then_inc(lanes_ready, 1)
            pool.iota(lane[:], [[1, NP]], base=0, channel_multiplier=0,
                      allow_small_or_imprecise_dtypes=True).then_inc(consts, 1)
            pool.memset(empty[:], 0.0).then_inc(pool_step, 1)
            pool.iota(tile0[:], [[NP, NT]], base=0, channel_multiplier=0,
                      allow_small_or_imprecise_dtypes=True).then_inc(consts, 1)
            pool.iota(tokid[:], [[NP, NT]], base=0, channel_multiplier=1,
                      allow_small_or_imprecise_dtypes=True).then_inc(consts, 1)
            pool.iota(rank[:], [[0, NT], [-1, NX]], base=NX, channel_multiplier=0,
                      allow_small_or_imprecise_dtypes=True).then_inc(consts, 1)
            lov = lo[:].rearrange("p (g r) -> p g r", r=CPT)
            hiv = hi[:].rearrange("p (g r) -> p g r", r=CPT)
            for v, r0, r1, base in ((lov, 0, MARGIN, -NP), (lov, MARGIN, CPT, 0),
                                    (hiv, 0, CPT - MARGIN, NP), (hiv, CPT - MARGIN, CPT, 2 * NP)):
                ins = pool.iota(v[:, :, r0:r1], [[NP, NT], [0, r1 - r0]], base=base, channel_multiplier=0,
                                allow_small_or_imprecise_dtypes=True)
            ins.then_inc(consts, 1)
            pool.wait_ge(pool_step, 3)
            pool.memset(empty[:, :, TOK], NOWHERE).then_inc(consts, 1)

            pool.wait_ge(dinv_ready, 1)
            pool.wait_ge(xw_copied, past(CG * TX))
            a, z = (CG - 1) * TX, CG * TX
            pool.tensor_tensor(Y[:, a:z, :], Y[:, a:z, :], dinv[:, a:z].unsqueeze(2).to_broadcast([NP, TX, D]),
                               ALU.mult).then_inc(y_scaled[CG - 1], 1)

            pool.wait_ge(table_stored, 16 * XG)

            def gather_half(half, i):
                hold(pool, idx_staged, 2 * i + half + 1)
                for r in range(CPT):
                    s = half * CPT + r
                    if not isinstance(i, int):
                        if r == 0:
                            hold(pool, batch_done, NB * (2 * i - 2 + half) + 1)
                        if r == MARGIN:
                            hold(pool, batch_done, NB * (2 * i - 2 + half) + 2)
                        if r == CPT - MARGIN:
                            hold(pool, batch_done, NB * (2 * i - 2 + half + 1) + 1)
                    pool.indirect_dma_start(
                        out=G[:, s, :], out_offset=None, in_=table,
                        in_offset=bass.IndirectOffsetOnAxis(ap=idx[:, s:s + 1], axis=0)).then_inc(gathered[s], 16)
            gather_half(0, 0)
            gather_half(1, 0)
            with pool.Fori(1, NT // 2) as i:
                gather_half(0, i)
                gather_half(1, i)
            last = NT // 2
            hold(pool, idx_staged, 2 * last + 1)
            for r in range(CPT):
                if r in (0, MARGIN):
                    hold(pool, batch_done, NB * (2 * last - 2) + 1 + r // MARGIN)
                if r == CPT - MARGIN:
                    hold(pool, batch_done, NB * (2 * last - 1) + 1)
                pool.indirect_dma_start(
                    out=G[:, r, :], out_offset=None, in_=table,
                    in_offset=bass.IndirectOffsetOnAxis(ap=idx[:, r:r + 1], axis=0)).then_inc(gathered[r], 16)

            pool.wait_ge(flag_ready, 1)
            late = pool.value_load(flag[0:1, 0:1], min_val=0, max_val=E)
            with pool.If(late > 0):
                with pool.Fori(0, NCH) as c:
                    hold(pool, fx_staged, c + 1)
                    pool.indirect_dma_start(
                        out=G[:, 0, :], out_offset=None, in_=table,
                        in_offset=bass.IndirectOffsetOnAxis(ap=fx_idx[:, 0:1], axis=0)).then_inc(fx_gathered, 16)

            pool.wait_ge(bn_rows, 1)
            for n, g in enumerate(BN_POOL):
                piece = Z[:, g * TX:(g + 1) * TX, :]
                pool.tensor_tensor(piece, piece, bnr[:, 2].unsqueeze(1).to_broadcast([NP, TX, D]),
                                   ALU.mult).then_inc(pool_step, 1)
                pool.wait_ge(pool_step, 4 + n)
                pool.tensor_tensor(piece, piece, bnr[:, 3].unsqueeze(1).to_broadcast([NP, TX, D]),
                                   ALU.add).then_inc(bn_part, 1)

            for t in range(NT):
                if owner(t) == "pool":
                    pool.wait_ge(nmr_ready, 2 + t // TX + 1)
                    pool.tensor_scalar(Y[:, t, :], X[:, t, :], rstd[:, t:t + 1], nmr[:, t:t + 1],
                                       ALU.mult, ALU.add).then_inc(h2_ready["pool"], 1)

            for n, (t0, t1) in enumerate(ROUTES):
                pool.wait_ge(slots_ready, n + 1)
                pool.wait_ge(probs_ready, n + 1)
                for who in h2_ready:
                    if h2_count(who, t1) > 0:
                        pool.wait_ge(h2_ready[who], h2_count(who, t1))
                for t in range(t0, t1):
                    if t == 0:
                        pool.wait_ge(empties_stored, 16 * NX)
                    pool.indirect_dma_start(
                        out=slots, out_offset=bass.IndirectOffsetOnAxis(ap=slot_i[:, t:t + 1], axis=0),
                        in_=XY[:, t, :], in_offset=None,
                        bounds_check=NX * SLOTS - 1, oob_is_err=False).then_inc(scattered, 16)

            pool.wait_ge(scattered, 16 * NT)
            pool.wait_ge(out_init, 16 * XG)

            def low_parts(e, b):
                for half, (a, z) in enumerate(HALVES):
                    hold(pool, w_hi_ready, 2 * e + half + 1)
                    pool.tensor_tensor(w_lo[b][:, a:z], raw[:, a:z], w_hi[b][:, a:z].bitcast(F32),
                                       ALU.subtract).then_inc(w_lo_ready, 1)

            def place_rows(e, b):
                hold(pool, y_ready, e + 1)
                for j in range(4):
                    pool.indirect_dma_start(
                        out=out, out_offset=bass.IndirectOffsetOnAxis(ap=tok_i[:, b, j:j + 1], axis=0),
                        in_=yb[:, b, j, :], in_offset=None,
                        bounds_check=N - 1, oob_is_err=False).then_inc(placed[b], 16)
            low_parts(1, 1)
            with pool.Fori(1, NX // 2) as i:
                for b in range(2):
                    low_parts(2 * i + b, b)
                    place_rows(2 * i - 2 + b, b)
            place_rows(NX - 2, 0)
            place_rows(NX - 1, 1)

        @block.scalar
        def _(act):
            for k in range(KD):
                act.dma_start(wcs[:, k, 0:D], conv_w[k * 128:(k + 1) * 128, :]).then_inc(wcs_ld, 16)
                act.dma_start(wcs[:, k, D:2 * D], self_w[k * 128:(k + 1) * 128, :]).then_inc(wcs_ld, 16)
            for c, v in enumerate((conv_b, self_b, gamma, beta)):
                act.dma_start(rows[:, c], v.rearrange("(a d) -> a d", a=1).to_broadcast([NP, D])).then_inc(rows_ld, 16)
            act.dma_start(wg[:], gate_w.rearrange("(k p) e -> p k e", p=128)).then_inc(gate_ld, 16)
            act.dma_start(gb[:], gate_b.rearrange("(e a) -> e a", a=1)).then_inc(gate_ld, 16)
            act.dma_start(b1r[:], b1.rearrange("e (f p) -> (e f) p", p=128)).then_inc(b1_ld, 16)
            for s in (hT_ready, xw_copied):
                act.sem_inc(s, CREDIT)

            act.wait_ge(consts, NCONST)
            for g in range(XG):
                act.wait_ge(var_ready, g + 1)
                act.activation(std[:, g * TX:(g + 1) * TX], mv[:, g * TX:(g + 1) * TX, 1], ACT.Sqrt,
                               bias=eps[0:NP, 0:1]).then_inc(std_ready, 1)

            def copy_hT(g, k):
                act.wait_ge(h_turned, past(TX * g + k + 1))
                act.wait_ge(xw_done, past(free(g, k)))
                turned = PS[:, H_BANKS[BUFFER[k]], 0:KD * NP].rearrange("p (k n) -> p k n", k=KD)
                act.activation(hT[:, BUFFER[k]], turned, ACT.Copy).then_inc(hT_ready, 1)

            def copy_xw(g, k, scaled):
                t = one(TX * g + k)
                act.wait_ge(xw_done, past(TX * g + k + 1))
                act.activation(Y[:, t, :].rearrange("p a d -> p (a d)"), PS[0:NP, W_BANKS[BUFFER[k]], 0:D], ACT.Copy,
                               scale=dinv[:, t] if scaled else 1.0).then_inc(xw_copied, 1)

            def first_lap(g, scaled):
                copy_hT(g, 0)
                for k in range(1, TX):
                    copy_hT(g, k)
                    copy_xw(g, k - 1, scaled)
                copy_xw(g, TX - 1, scaled)
            with act.Fori(0, CG) as g:
                first_lap(g, False)

            act.wait_ge(erow_turned, 2)
            act.activation(srcT[:], PS[0:NP, 0, 0:NCH], ACT.Copy).then_inc(src_ready, 1)
            act.wait_ge(src_ready, 1)

            def stage(i, half, first=False):
                if not first:
                    for s in range(half * CPT, (half + 1) * CPT):
                        act.wait_ge(gathered[s], 16 * i)
                act.activation(idx[:, half * CPT:(half + 1) * CPT],
                               srcT[:, bass.ds(RING * i + half * CPT, CPT)], ACT.Copy).then_inc(idx_staged, 1)
            stage(0, 0, True)
            stage(0, 1, True)

            act.wait_ge(deg_counted, DB + NDEG)
            act.activation(sqdeg[:], PS[0:NT, 2, 0:NP], ACT.Sqrt).then_inc(degsqrt, 1)
            act.wait_ge(dinv_ready, 1)
            for g in range(CG, XG):
                first_lap(g, True)

            def layernorm(g, first, k):
                act.wait_ge(h_turned, past(TX * (g - 1) + k + 1))
                t = one(first + k)
                act.activation(h5[:, k], X[:, t, :].rearrange("p a d -> p (a d)"), ACT.Identity, bias=nmr[:, t],
                               scale=rstd[:, t]).then_inc(h_ready, 1)
            act.wait_ge(nmr_ready, 1)
            for k in range(TX):
                layernorm(XG, 0, k)


            act.wait_ge(b1_turned, 1)
            act.activation(b1c[:], PS[:, 0, 0:NX * KF], ACT.Copy).then_inc(b1_ready, 1)

            def copy_self(g, first, k):
                act.wait_ge(xw_done, past(TX * g + k + 1))
                act.activation(Z[:, one(first + k), :].rearrange("p a d -> p (a d)"), PS[0:NP, W_BANKS[BUFFER[k]], 0:D],
                               ACT.Copy).then_inc(xw_copied, 1)

            def second_lap(g, first, last=False):
                for k in range(TX):
                    if k + 1 < TX:
                        copy_hT(g, k + 1)
                    elif not last:
                        copy_hT(g + 1, 0)
                    copy_self(g, first, k)
                    if not last:
                        layernorm(g + 1, first + TX, k)
            copy_hT(XG, 0)
            with act.Fori(XG, 2 * XG - 1) as g:
                second_lap(g, TX * (g - XG))
            second_lap(2 * XG - 1, NT - TX, last=True)

            def high_parts(e, b):
                for half, (a, z) in enumerate(HALVES):
                    act.wait_ge(raw_ld[half], 16 * (e + 1))
                    act.activation(w_hi[b][:, a:z], raw[:, a:z], ACT.Copy).then_inc(w_hi_ready, 1)
            def square(t, b, done):
                act.wait_ge(dev_ready, t + 1)
                act.activation(dev[:, b, 1], dev[:, b, 0], ACT.Square).then_inc(done, 1)

            def two_squares(i):
                stage(i, 0)
                square(2 * i - 2, 0, squared)
                stage(i, 1)
                square(2 * i - 1, 1, squared)
            two_squares(1)
            act.wait_ge(missed, 1)
            high_parts(0, 0)
            with act.Fori(2, NT // 2) as i:
                two_squares(i)
            stage(NT // 2, 0)
            square(NT - 3, 0, squared)
            square(NT - 2, 1, squared)
            square(NT - 1, 0, squared)
            act.wait_ge(flag_ready, 1)
            late = act.value_load(flag[0:1, 0:1], min_val=0, max_val=E)
            with act.If(late > 0):
                with act.Fori(0, NT) as t:
                    act.wait_ge(fx_dev, t + 1)
                    act.activation(dev[:, 0, 1], dev[:, 0, 0], ACT.Square).then_inc(fx_squared, 1)

            act.wait_ge(bn_scale, 1)
            act.activation(bnr[:, 1], bnr[:, 0], ACT.Sqrt, bias=eps[0:NP, 0:1]).then_inc(bnstd, 1)

            act.wait_ge(gate_ld, 32)

            def copy_h2T(t):
                act.wait_ge(h2_turned, t + 1)
                if t >= TB:
                    act.wait_ge(logits_done, t - TB + 1)
                act.activation(hT[:, t % TB], PS[:, T_BANKS[t % TB], 0:KD * NP].rearrange("p (k n) -> p k n", k=KD),
                               ACT.Copy).then_inc(h2T_ready, 1)

            def copy_logits(q):
                n = min(LG, NT - LG * q)
                act.wait_ge(logits_done, LG * q + n)
                if q >= 2:
                    act.wait_ge(logits_turned, q - 1)
                act.activation(lgT[:, q % 2, 0:n * NP], PS[0:NX, E_BANKS[q % 2], 0:n * NP], ACT.Identity,
                               bias=gb[:]).then_inc(logits_copied, 1)

            def exp_part(n):
                t0, t1 = ROUTES[n]
                act.wait_ge(shifted, n + 1)
                act.activation(t8b[:, t0:t1], t8a[:, t0:t1], ACT.Exp).then_inc(exped, 1)

            def copy_tile(t):
                copy_h2T(t)
                if t % LG == AFTER - 1 and t >= LG:
                    copy_logits(t // LG - 1)
                if t in EXPS:
                    exp_part(EXPS[t])
            AFTER = 2
            for g in range(XG):
                act.wait_ge(var2_ready, g + 1)
                act.activation(std[:, g * TX:(g + 1) * TX], mv[:, g * TX:(g + 1) * TX, 1], ACT.Sqrt,
                               bias=eps[0:NP, 0:1]).then_inc(std2_ready, 1)
                if g >= 1:
                    for t in range((g - 1) * TX, g * TX):
                        copy_tile(t)
                if g < XG - 1:
                    act.wait_ge(nmr_ready, 2 + g + 1)
                for t in range(g * TX, (g + 1) * TX):
                    if owner(t) == "act":
                        act.activation(Y[:, t, :], X[:, t, :], ACT.Identity, bias=nmr[:, t:t + 1],
                                       scale=rstd[:, t:t + 1]).then_inc(h2_ready["act"], 1)

            for t in range((XG - 1) * TX, NT):
                copy_tile(t)
            for q in range(NQ - 2, NQ):
                copy_logits(q)
            exp_part(len(ROUTES) - 1)

            act.wait_ge(b1_ready, 1)

            def high_rows(e):
                act.wait_ge(r_turned, e + 1)
                act.activation(buf_hi[:], PS[:, 0:KD, 0:SC], ACT.Copy).then_inc(buf_hi_ready, 1)

            def hidden(e):
                for f in range(KF):
                    act.wait_ge(hid_done, KF * e + f + 1)
                    act.wait_ge(hid_lo_ready, past(KF * e + f - 1) if f >= 2 else past(KF * e))
                    act.activation(hid[:, f % 2], PS[:, 2 + f % 2, 0:SC], ACT.Relu,
                                   bias=b1c[:, one(KF * e + f)]).then_inc(hid_relu, 1)
                    act.wait_ge(hid_relu, KF * e + f + 1)
                    act.wait_ge(ffn_done, past(e))
                    act.activation(hid_hi[:, f], hid[:, f % 2], ACT.Copy).then_inc(hid_hi_ready, 1)
            high_rows(0)
            act.wait_ge(scattered, 16 * NT)
            act.wait_ge(out_init, 16 * XG)
            hidden(0)
            high_parts(1, 1)
            high_rows(1)
            with act.Fori(1, NX // 2) as i:
                for b in range(2):
                    hidden(2 * i - 1 + b)
                    high_rows(2 * i + b)
                    high_parts(2 * i + b, b)
            hidden(NX - 1)

        @block.tensor
        def _(pe):
            for s in (h_turned, xw_done, ffn_done):
                pe.sem_inc(s, CREDIT)
            pe.sem_inc(deg_counted, DB)
            pe.wait_ge(ident_ready, 1)
            idn = ident[0:NP, 0:NP]

            def turn_edges(which):
                pe.wait_ge(erow_conv, which + 1)
                for k in range(NG):
                    mm = pe.transpose(PS[0:NP, 0, k * GRP:(k + 1) * GRP], erow_f[:, which, k],
                                      ident[0:GRP, 0:GRP])
                mm.then_inc(erow_turned, 1)
            turn_edges(0)

            def turn_h(g, k):
                pe.wait_ge(h_ready, TX * g + k + 1)
                pe.wait_ge(hT_ready, past(free(g, k)))
                for c in range(KD):
                    mm = pe.transpose(PS[:, H_BANKS[BUFFER[k]], c * NP:(c + 1) * NP],
                                      h5[:, k, c * 128:(c + 1) * 128], idn)
                mm.then_inc(h_turned, 1)

            def times_w(g, k, which):
                pe.wait_ge(hT_ready, past(TX * g + k + 1))
                pe.wait_ge(xw_copied, past(free(g, k)))
                for c in range(KD):
                    mm = pe.matmul(PS[0:NP, W_BANKS[BUFFER[k]], 0:D], hT[:, BUFFER[k], c],
                                   wcs[:, c, which * D:(which + 1) * D],
                                   start=(c == 0), stop=(c == KD - 1))
                mm.then_inc(xw_done, 1)

            def count(g, b):
                pe.wait_ge(onehot_deg, DPG * g + b + 1)
                for k in range(DC):
                    mm = pe.matmul(PS[0:NT, 2, 0:NP], onq[:, b % DB, :, k], onr[:, b % DB, :, k],
                                   start=False, stop=False, skip_group_check=True)
                mm.then_inc(deg_counted, 1)
            pe.wait_ge(consts, NCONST)
            pe.matmul(PS[0:NT, 2, 0:NP], ones[0:1, 0:NT], ones[0:1, :], start=True, stop=False, skip_group_check=True)
            turn_edges(1)
            pe.wait_ge(wcs_ld, 16 * 2 * KD)

            def first_lap(g, counting=False):
                turn_h(g, 0)
                for k in range(TX):
                    if k + 1 < TX:
                        turn_h(g, k + 1)
                    times_w(g, k, 0)
                    if counting and k >= TX - DPG:
                        count(g, k - (TX - DPG))
            with pe.Fori(0, CG) as g:
                first_lap(g, counting=True)
            pe.wait_ge(degsqrt, 1)
            pe.transpose(PS[0:NP, 2, 0:NT], sqdeg[:], ident[0:NT, 0:NT]).then_inc(degsqrt_turned, 1)
            for g in range(CG, XG):
                first_lap(g)
            pe.wait_ge(b1_ld, 16)
            pe.wait_ge(src_ready, 1)
            pe.transpose(PS[:, 0, 0:NX * KF], b1r[:], ident[0:NX * KF, 0:NX * KF]).then_inc(b1_turned, 1)
            turn_h(XG, 0)

            def second_lap(g, last=False):
                for k in range(TX):
                    if k + 1 < TX:
                        turn_h(g, k + 1)
                    elif not last:
                        turn_h(g + 1, 0)
                    times_w(g, k, 1)
            with pe.Fori(XG, 2 * XG - 1) as g:
                second_lap(g)
            second_lap(2 * XG - 1, last=True)

            pe.wait_ge(dinv_ready, 1)

            pe.wait_ge(b1_ready, 1)

            def aggregate(t, par, start, skip, end, wraps):
                for b in range(NB):
                    pe.wait_ge(onehots, NB * t + b + 1)
                    for k in range(b * BATCH, (b + 1) * BATCH):
                        if k < skip or k >= end:
                            continue
                        c = start + k
                        pe.wait_ge(gathered[c % RING], 16 * (wraps + c // RING + 1))
                        if k == skip:
                            if not isinstance(t, int) or t >= 2:
                                pe.wait_ge(z_done, t - 1)
                        mm = pe.matmul(PS[0:NP, par, 0:D], OH[:, k], G[:, c % RING, :],
                                       start=(k == skip), stop=(k == end - 1))
                    mm.then_inc(batch_done, 1)

            def sum_dev(t, b, ready, stop=False):
                pe.wait_ge(ready, t + 1)
                for c in range(2):
                    mm = pe.matmul(PS[0:NP, 2 + c, 0:D], ones[:], dev[:, b, c], start=False, stop=stop,
                                   skip_group_check=True)
                return mm

            def zero_sums():
                for c in range(2):
                    pe.matmul(PS[0:NP, 2 + c, 0:D], nought[:], rows[:, 0], start=True, stop=False,
                              skip_group_check=True)
            half = CPT - MARGIN
            aggregate(0, 0, -MARGIN, MARGIN, WIN, 0)
            aggregate(1, 1, half, 0, WIN, 0)
            pe.wait_ge(z_done, 1)
            pe.matmul(PS[0:NP, 7, 0:D], ones[:], Z[:, 0, :], start=True, stop=True).then_inc(tile_summed, 1)
            zero_sums()

            def two_tiles(i):
                aggregate(2 * i, 0, -MARGIN, 0, WIN, i)
                sum_dev(2 * i - 2, 0, squared).then_inc(dev_summed, 1)
                aggregate(2 * i + 1, 1, half, 0, WIN, i)
                sum_dev(2 * i - 1, 1, squared).then_inc(dev_summed, 1)
            two_tiles(1)
            pe.wait_ge(missed, 1)
            pe.matmul(PS[0:1, 7, 0:1], ones[:, 0:1], missing[:], start=True, stop=True).then_inc(missed_sum, 1)
            with pe.Fori(2, NT // 2) as i:
                two_tiles(i)
            aggregate(NT - 1, 0, -MARGIN, 0, CPT + MARGIN, NT // 2)
            sum_dev(NT - 3, 0, squared).then_inc(dev_summed, 1)
            sum_dev(NT - 2, 1, squared).then_inc(dev_summed, 1)
            sum_dev(NT - 1, 0, squared, stop=True).then_inc(dev_summed, 1)

            pe.wait_ge(flag_ready, 1)
            late = pe.value_load(flag[0:1, 0:1], min_val=0, max_val=E)
            with pe.If(late > 0):
                with pe.Fori(0, NCH) as c:
                    with pe.Fori(0, NT) as t:
                        pe.wait_ge(fx_gathered, 16 * (c + 1))
                        pe.wait_ge(fx_onehot, NT * c + t + 1)
                        pe.matmul(PS[0:NP, 4, 0:D], OH[:, 0], G[:, 0, :], start=True, stop=True).then_inc(fx_mm, 1)
                zero_sums()
                with pe.Fori(0, NT) as t:
                    sum_dev(t, 0, fx_squared).then_inc(fx_summed, 1)

            pe.wait_ge(gate_ld, 32)

            def turn_h2(t):
                pe.wait_ge(h2_ready[owner(t)], h2_count(owner(t), t + 1))
                if t >= TB:
                    pe.wait_ge(h2T_ready, t - TB + 1)
                for k in range(KD):
                    mm = pe.transpose(PS[:, T_BANKS[t % TB], k * NP:(k + 1) * NP], Y[:, t, k * 128:(k + 1) * 128], idn)
                mm.then_inc(h2_turned, 1)

            def logits(t):
                q, n = t // LG, t % LG
                pe.wait_ge(h2T_ready, t + 1)
                if n == 0 and q >= 2:
                    pe.wait_ge(logits_copied, q - 1)
                for k in range(KD):
                    mm = pe.matmul(PS[0:NX, E_BANKS[q % 2], n * NP:(n + 1) * NP], wg[:, k], hT[:, t % TB, k],
                                   start=(k == 0), stop=(k == KD - 1))
                mm.then_inc(logits_done, 1)

            def turn_logits(q):
                pe.wait_ge(logits_copied, q + 1)
                for t in range(LG * q, min(NT, LG * (q + 1))):
                    bank = next(b for b, (_, t1) in zip(L_BANKS, ROUTES) if t < t1)
                    mm = pe.transpose(PS[0:NP, bank, t * NX:(t + 1) * NX],
                                      lgT[:, q % 2, (t % LG) * NP:(t % LG + 1) * NP], ident[0:NX, 0:NX])
                mm.then_inc(logits_turned, 1)

            def count_tokens(n):
                t0, t1 = ROUTES[n]
                pe.wait_ge(picked, n + 1)
                counts = PS[0:NP, 0, 0:NT * NX].rearrange("p (t e) -> p t e", e=NX)
                pe.matmul(counts[:, t0:t1], upper[:], pick[:, t0:t1], start=True, stop=False, skip_group_check=True)
                for t in range(t1 - 1):
                    a = max(t + 1, t0)
                    mm = pe.matmul(counts[:, a:t1], ones_bf[:], pick[:, t].unsqueeze(1).to_broadcast([NP, t1 - a, NX]),
                                   start=False, stop=(t == t1 - 2), skip_group_check=True)
                mm.then_inc(counted, 1)
            for t in range(NT):
                turn_h2(t)
                if t >= TB - 1:
                    done = t - TB + 1
                    logits(done)
                    if done % LG == 1 and done >= LG:
                        turn_logits(done // LG - 1)
                if t in COUNTS:
                    count_tokens(COUNTS[t])
            for t in range(NT - TB + 1, NT):
                logits(t)
            for q in range(NQ - 2, NQ):
                turn_logits(q)
            count_tokens(len(ROUTES) - 1)

            def turn_rows(e, i, b):
                pe.wait_ge(r_ld[b], 16 * (i + 1))
                for j in range(4):
                    for k in range(KD):
                        mm = pe.transpose(PS[:, k, j * SP4:(j + 1) * SP4], R[:, b, j, k * 128:(k + 1) * 128],
                                          ident[0:SP4, 0:SP4])
                mm.then_inc(r_turned, 1)

            def hidden(e, b):
                pe.wait_ge(buf_hi_ready, e + 1)
                pe.wait_ge(buf_lo_ready, e + 1)
                pe.wait_ge(w_hi_ready, 2 * e + 1)
                pe.wait_ge(w_lo_ready, 2 * e + 1)
                h, l = w1_of(w_hi[b]), w1_of(w_lo[b])
                for f in range(KF):
                    cols = slice(f * 128, (f + 1) * 128)
                    if f >= 2:
                        pe.wait_ge(hid_relu, KF * e + f - 1)
                    for k in range(KD):
                        pe.matmul(PS[:, 2 + f % 2, 0:SC], h[:, k, cols], buf_hi[:, k], start=(k == 0), stop=False)
                        pe.matmul(PS[:, 2 + f % 2, 0:SC], h[:, k, cols], buf_lo[:, k], start=False, stop=False)
                        mm = pe.matmul(PS[:, 2 + f % 2, 0:SC], l[:, k, cols], buf_hi[:, k],
                                       start=False, stop=(k == KD - 1))
                    mm.then_inc(hid_done, 1)

            def results(e, b):
                pe.wait_ge(w_hi_ready, 2 * e + 2)
                pe.wait_ge(w_lo_ready, 2 * e + 2)
                pe.wait_ge(y_copied, past(4 * e))
                h, l = w2_of(w_hi[b]), w2_of(w_lo[b])
                for f in range(KF):
                    pe.wait_ge(hid_lo_ready, past(KF * e + f + 1))
                    for j in range(4):
                        cols = slice(j * SP4, (j + 1) * SP4)
                        o = PS[0:SP4, 4 + j, 0:D]
                        pe.matmul(o, hid_hi[:, f, cols], h[:, f], start=(f == 0), stop=False)
                        pe.matmul(o, hid_hi[:, f, cols], l[:, f], start=False, stop=False)
                        mm = pe.matmul(o, hid_lo[:, f, cols], h[:, f], start=False, stop=(f == KF - 1))
                mm.then_inc(ffn_done, 1)
            turn_rows(0, 0, 0)
            hidden(0, 0)
            turn_rows(1, 0, 1)
            results(0, 0)
            with pe.Fori(1, NX // 2) as i:
                hidden(2 * i - 1, 1)
                turn_rows(2 * i, i, 0)
                results(2 * i - 1, 1)
                hidden(2 * i, 0)
                turn_rows(2 * i + 1, i, 1)
                results(2 * i, 0)
            hidden(NX - 1, 1)
            results(NX - 1, 1)

        @block.vector
        def _(dve):
            done = [0]

            def link(ins):
                done[0] += 1
                ins.then_inc(dve_step, 1)
                dve.wait_ge(dve_step, done[0])

            def flat(a):
                return a.rearrange("p a d -> p (a d)")

            for s in (y_copied, hid_lo_ready):
                dve.sem_inc(s, CREDIT)
            dve.sem_inc(yb_free, 2)
            dve.wait_ge(dst_ld, 16)
            dve.tensor_copy(erow_f[:, 0], erow[:, 0]).then_inc(erow_conv, 1)

            def layer_stats(g, ready):
                for t in range(g * TX, (g + 1) * TX):
                    ins = dve.bn_stats(stats[:, t], X[:, t, :])
                link(ins)
                for t in range(g * TX, (g + 1) * TX):
                    ins = dve.bn_aggr(mv[:, t], stats[:, t])
                ins.then_inc(ready, 1)

            def layer_rstd(g, root):
                dve.wait_ge(root, g + 1)
                return dve.reciprocal(rstd[:, g * TX:(g + 1) * TX], std[:, g * TX:(g + 1) * TX])
            for g in range(XG):
                dve.wait_ge(x_ld[g], 16)
                layer_stats(g, var_ready)
                if g == 0:
                    dve.wait_ge(erow_turned, 1)
                    link(dve.tensor_copy(dstT[:], PS[0:NP, 0, 0:NCH]))
                    link(dve.tensor_scalar(qf[:], dstT[:], 1.0 / NP, 0.5 / NP - 0.5, ALU.mult, ALU.add))
                    link(dve.tensor_scalar(rf[:], qf[:], ROUND, None, ALU.add))
                    link(dve.tensor_scalar(qf[:], rf[:], ROUND, None, ALU.subtract))
                    dve.tensor_copy(q_bf[:], qf[:])
                    link(dve.scalar_tensor_tensor(out=r_bf[:], in0=qf[:], scalar=-float(NP), in1=dstT[:],
                                                  op0=ALU.mult, op1=ALU.add))
                if g == 1:
                    dve.wait_ge(src_ld, 16)
                    dve.tensor_copy(erow_f[:, 1], erow[:, 1]).then_inc(erow_conv, 1)
                if g >= 1:
                    layer_rstd(g - 1, std_ready).then_inc(rstd_ready, TX)
            layer_rstd(XG - 1, std_ready).then_inc(rstd_ready, TX)
            dve.wait_ge(lanes_ready, 1)
            dve.wait_ge(rstd_ready, NT)
            dve.scalar_tensor_tensor(out=nmr[:], in0=mv[:, :, 0], scalar=-1.0, in1=rstd[:], op0=ALU.mult,
                                     op1=ALU.mult).then_inc(nmr_ready, 1)
            dve.tensor_scalar(rstd1[:], rstd[:], 1.0, None, ALU.add).then_inc(nmr_ready, 1)

            def layernorm(g, first):
                dve.wait_ge(h_turned, past(TX * g))
                for k in range(TX):
                    dve.tensor_scalar(h5[:, k], flat(X[:, one(first + k), :]), mv[:, one(first + k), 0],
                                      rstd[:, one(first + k)], ALU.subtract, ALU.mult).then_inc(h_ready, 1)
            with dve.Fori(0, CG) as g:
                layernorm(g, TX * g)
                for b in range(DPG):
                    dve.wait_ge(deg_counted, DPG * g + b + 1)
                    c = bass.ds(DC * (DPG * g + b), DC)
                    dve.tensor_tensor(onq[:, b % DB], q_bf[:, c].unsqueeze(1).to_broadcast([NP, NT, DC]),
                                      lanes[:, 0:NT], ALU.is_equal)
                    dve.tensor_tensor(onr[:, b % DB], r_bf[:, c].unsqueeze(1).to_broadcast([NP, NP, DC]), lanes[:],
                                      ALU.is_equal).then_inc(onehot_deg, 1)
            layernorm(CG, TX * CG)

            dve.wait_ge(degsqrt_turned, 1)
            dve.reciprocal(dinv[:], PS[0:NP, 2, 0:NT]).then_inc(dinv_ready, 1)
            dve.wait_ge(dinv_ready, 1)
            dve.wait_ge(xw_copied, past((CG - 1) * TX))
            for g in range(CG - 1):
                a, z = g * TX, (g + 1) * TX
                dve.tensor_tensor(Y[:, a:z, :], Y[:, a:z, :], dinv[:, a:z].unsqueeze(2).to_broadcast([NP, TX, D]),
                                  ALU.mult).then_inc(y_scaled[g], 1)

            def onehot_tile(t, par, skip, end, first=False):
                n = end - skip
                dve.tensor_scalar(dloc[:, par, skip:end], dstT[:, bass.ds(CPT * t - MARGIN + skip, n)],
                                  tile0[:, one(t)], None, ALU.subtract).then_inc(dloc_ready, 1)
                dve.wait_ge(dloc_ready, t + 1)
                for b in range(NB):
                    if not first:
                        dve.wait_ge(batch_done, NB * (t - 1) + b + 1)
                    for k in range(max(skip, b * BATCH), min(end, (b + 1) * BATCH)):
                        ins = dve.tensor_scalar(OH[:, k], lane[:], dloc[:, par, k:k + 1], None, ALU.is_equal)
                    ins.then_inc(onehots, 1)

            onehot_tile(0, 0, MARGIN, WIN, first=True)

            dve.wait_ge(nmr_ready, 2)
            dve.wait_ge(rows_ld, 64)
            link(dve.tensor_tensor(bnr[:, 0], rows[:, 0], rows[:, 1], ALU.add))
            with dve.Fori(XG, 2 * XG) as g:
                first = TX * (g - XG)
                dve.wait_ge(h_ready, TX * (g + 1))
                for k in range(TX):
                    t = one(first + k)
                    ins = dve.tensor_scalar(flat(X[:, t, :]), flat(X[:, t, :]), rstd1[:, t], nmr[:, t],
                                            ALU.mult, ALU.add)
                ins.then_inc(xh_ready, 1)
                dve.wait_ge(xw_copied, past(TX * (g + 1)))
                piece = Z[:, bass.ds(first, TX), :]
                dve.tensor_tensor(piece, piece, bnr[:, 0].unsqueeze(1).to_broadcast([NP, TX, D]), ALU.add) \
                   .then_inc(z_biased, 1)
            for g in range(CG):
                dve.wait_ge(y_scaled[g], 1)
            dve.wait_ge(z_biased, XG)

            def own_messages(t):
                dve.scalar_tensor_tensor(out=flat(Z[:, one(t), :]), in0=flat(Y[:, one(t), :]), scalar=dinv[:, one(t)],
                                         in1=flat(Z[:, one(t), :]), op0=ALU.mult, op1=ALU.add).then_inc(own_added, 1)

            def finish_tile(t, par):
                dve.wait_ge(own_added, t + 1)
                dve.wait_ge(batch_done, NB * (t + 1))
                dve.scalar_tensor_tensor(out=flat(Z[:, one(t), :]), in0=PS[0:NP, par, 0:D], scalar=dinv[:, one(t)],
                                         in1=flat(Z[:, one(t), :]), op0=ALU.mult, op1=ALU.add).then_inc(z_done, 1)
            def deviate(t, b, first=False):
                if not first:
                    dve.wait_ge(dev_summed, t - 1)
                dve.tensor_tensor(dev[:, b, 0], flat(Z[:, one(t), :]), shift[:], ALU.subtract).then_inc(dev_ready, 1)
            dve.memset(nought[:], 0.0)
            link(dve.memset(XY[:, :, D:RES], 0.0))
            link(dve.tensor_copy(XY[:, :, TOK], tokid[:]))
            own_messages(0)
            onehot_tile(1, 1, 0, WIN)
            own_messages(1)
            finish_tile(0, 0)
            onehot_tile(2, 0, 0, WIN)
            own_messages(2)
            finish_tile(1, 1)
            dve.wait_ge(tile_summed, 1)
            link(dve.tensor_scalar(shift[:], PS[0:NP, 7, 0:D], 1.0 / NP, None, ALU.mult))
            dve.wait_ge(z_done, 2)
            deviate(0, 0, True)
            deviate(1, 1, True)
            onehot_tile(3, 1, 0, WIN)
            own_messages(3)
            finish_tile(2, 0)

            link(dve.tensor_tensor(rf[:], dstT[:], lo[:], ALU.is_lt))
            link(dve.tensor_tensor(qf[:], dstT[:], hi[:], ALU.is_ge))
            link(dve.tensor_tensor(rf[:], rf[:], qf[:], ALU.add))
            dve.reduce_sum(missing[:], rf[:], axis=AX_X).then_inc(missed, 1)
            link(dve.scalar_tensor_tensor(out=qf[:], in0=dstT[:], scalar=1.0, in1=rf[:], op0=ALU.add, op1=ALU.mult))
            link(dve.tensor_scalar(qf[:], qf[:], -1.0, None, ALU.add))

            def next_tile(t, b):
                onehot_tile(t, b, 0, WIN)
                own_messages(t)
                finish_tile(t - 1, 1 - b)
                dve.wait_ge(z_done, t - 1)
                deviate(t - 2, b)
            for half, (a, z) in enumerate(HALVES):
                next_tile(4 + half, half)
                dve.wait_ge(w_hi_ready, half + 1)
                dve.tensor_tensor(w_lo[0][:, a:z], raw[:, a:z], w_hi[0][:, a:z].bitcast(F32),
                                  ALU.subtract).then_inc(w_lo_ready, 1)
            with dve.Fori(3, NT // 2) as i:
                for b in range(2):
                    next_tile(2 * i + b, b)
            dve.wait_ge(missed_sum, 1)
            dve.tensor_copy(flag[:], PS[0:1, 7, 0:1]).then_inc(flag_ready, 1)
            onehot_tile(NT - 1, 0, 0, CPT + MARGIN)
            own_messages(NT - 1)
            finish_tile(NT - 2, 1)
            dve.wait_ge(z_done, NT - 1)
            deviate(NT - 3, 0)
            deviate(NT - 2, 1)
            finish_tile(NT - 1, 0)
            dve.wait_ge(z_done, NT)
            deviate(NT - 1, 0)

            late = dve.value_load(flag[0:1, 0:1], min_val=0, max_val=E)
            with dve.If(late > 0):
                with dve.Fori(0, NCH) as c:
                    dve.tensor_scalar(fx_loc[:], tile0[:], -1.0, qf[:, one(c)], ALU.mult, ALU.add) \
                       .then_inc(fx_located, 1)
                    dve.tensor_copy(fx_idx[:], srcT[:, one(c)]).then_inc(fx_staged, 1)
                    with dve.Fori(0, NT) as t:
                        dve.wait_ge(fx_located, c + 1)
                        dve.tensor_scalar(OH[:, 0], lane[:], fx_loc[:, one(t)], None, ALU.is_equal) \
                           .then_inc(fx_onehot, 1)
                        dve.wait_ge(fx_mm, NT * c + t + 1)
                        dve.scalar_tensor_tensor(out=flat(Z[:, one(t), :]), in0=PS[0:NP, 4, 0:D],
                                                 scalar=dinv[:, one(t)], in1=flat(Z[:, one(t), :]),
                                                 op0=ALU.mult, op1=ALU.add).then_inc(fx_added, 1)
                        dve.wait_ge(fx_added, NT * c + t + 1)
                dve.wait_ge(dev_summed, NT)
                with dve.Fori(0, NT) as t:
                    dve.tensor_tensor(dev[:, 0, 0], flat(Z[:, one(t), :]), shift[:], ALU.subtract).then_inc(fx_dev, 1)
                    hold(dve, fx_summed, t + 1)

            dve.wait_ge(dev_summed, NT)
            link(dve.tensor_scalar(bnr[:, 3], PS[0:NP, 2, 0:D], 1.0 / N, None, ALU.mult))
            dve.tensor_tensor(shift[:], shift[:], bnr[:, 3], ALU.add)
            link(dve.tensor_tensor(bnr[:, 2], bnr[:, 3], bnr[:, 3], ALU.mult))
            dve.scalar_tensor_tensor(out=bnr[:, 0], in0=PS[0:NP, 3, 0:D], scalar=1.0 / N, in1=bnr[:, 2],
                                     op0=ALU.mult, op1=ALU.subtract).then_inc(bn_scale, 1)
            dve.wait_ge(bnstd, 1)
            link(dve.reciprocal(bnr[:, 2], bnr[:, 1]))
            link(dve.tensor_tensor(bnr[:, 2], bnr[:, 2], rows[:, 2], ALU.mult))
            link(dve.tensor_tensor(bnr[:, 3], shift[:], bnr[:, 2], ALU.mult))
            dve.tensor_tensor(bnr[:, 3], rows[:, 3], bnr[:, 3], ALU.subtract).then_inc(bn_rows, 1)
            dve.wait_ge(bn_rows, 1)

            def layer_norms(g):
                link(layer_rstd(g, std2_ready))
                a, z = g * TX, (g + 1) * TX
                dve.scalar_tensor_tensor(out=nmr[:, a:z], in0=mv[:, a:z, 0], scalar=-1.0, in1=rstd[:, a:z],
                                         op0=ALU.mult, op1=ALU.mult).then_inc(nmr_ready, 1)
            def scale_and_shift(g):
                piece = Z[:, g * TX:(g + 1) * TX, :]
                link(dve.tensor_tensor(piece, piece, bnr[:, 2].unsqueeze(1).to_broadcast([NP, TX, D]), ALU.mult))
                link(dve.tensor_tensor(piece, piece, bnr[:, 3].unsqueeze(1).to_broadcast([NP, TX, D]), ALU.add))
            scale_and_shift(0)
            for g in range(XG):
                a, z = g * TX, (g + 1) * TX
                if g in BN_POOL:
                    dve.wait_ge(bn_part, g - BN_POOL[0] + 1)
                dve.scalar_tensor_tensor(out=X[:, a:z, :], in0=Z[:, a:z, :], scalar=0.0, in1=X[:, a:z, :],
                                         op0=ALU.max, op1=ALU.add).then_inc(x2_ready, 1)
                dve.wait_ge(x2_ready, g + 1)
                layer_stats(g, var2_ready)
                if g >= 1:
                    layer_norms(g - 1)
                if g == 1:
                    scale_and_shift(XG - 1)
            counts = PS[0:NP, 0, 0:NT * NX].rearrange("p (t e) -> p t e", e=NX)

            def choose(n):
                t0, t1 = ROUTES[n]
                best, chosen = v25[:, 0, t0:t1], v25[:, 1, t0:t1]

                def wide(a):
                    return a.unsqueeze(2).to_broadcast([NP, t1 - t0, NX])
                logit = PS[0:NP, L_BANKS[n], 0:NT * NX].rearrange("p (t e) -> p t e", e=NX)[:, t0:t1]
                work, picks = lg[:, t0:t1], pick[:, t0:t1]
                dve.wait_ge(logits_turned, ceil(t1 / LG))
                link(dve.tensor_reduce(best, logit, AX_X, ALU.max))
                dve.tensor_tensor(t8a[:, t0:t1], logit, wide(best), ALU.subtract).then_inc(shifted, 1)
                link(dve.tensor_tensor(work, logit, wide(best), ALU.is_equal))
                link(dve.tensor_tensor(work, work, rank[:, t0:t1], ALU.mult))
                link(dve.tensor_reduce(chosen, work, AX_X, ALU.max))
                dve.tensor_tensor(picks, work, wide(chosen), ALU.is_equal).then_inc(picked, 1)

            def place(n):
                t0, t1 = ROUTES[n]
                chosen, place, lost = (v25[:, c, t0:t1] for c in range(1, 4))
                work, picks = lg[:, t0:t1], pick[:, t0:t1]
                dve.wait_ge(picked, n + 1)
                dve.wait_ge(counted, n + 1)
                link(dve.tensor_tensor(work, counts[:, t0:t1], picks, ALU.mult))
                link(dve.tensor_reduce(place, work, AX_X, ALU.add))
                dve.tensor_scalar(lost, place, float(CAP), NOWHERE, ALU.is_gt, ALU.mult)
                link(dve.scalar_tensor_tensor(out=place, in0=chosen, scalar=-float(SLOTS), in1=place,
                                              op0=ALU.mult, op1=ALU.add))
                dve.scalar_tensor_tensor(out=slot_i[:, t0:t1], in0=place, scalar=float(NX * SLOTS - 1), in1=lost,
                                         op0=ALU.add, op1=ALU.add).then_inc(slots_ready, 1)

            def probabilities(n):
                t0, t1 = ROUTES[n]
                dve.wait_ge(exped, n + 1)
                link(dve.tensor_reduce(v25[:, 4, t0:t1], t8b[:, t0:t1], AX_X, ALU.add))
                dve.reciprocal(XY[:, t0:t1, PRB], v25[:, 4, t0:t1]).then_inc(probs_ready, 1)
            choose(0)
            place(0)
            layer_norms(XG - 1)
            dve.wait_ge(nmr_ready, 2 + XG)
            for t in range(NT):
                if owner(t) == "dve":
                    dve.tensor_scalar(Y[:, t, :], X[:, t, :], rstd[:, t:t + 1], nmr[:, t:t + 1],
                                      ALU.mult, ALU.add).then_inc(h2_ready["dve"], 1)
            probabilities(0)
            for n in range(1, len(ROUTES)):
                choose(n)
                place(n)
                probabilities(n)

            def low_rows(e):
                dve.wait_ge(buf_hi_ready, e + 1)
                dve.tensor_tensor(buf_lo[:], PS[:, 0:KD, 0:SC], buf_hi[:].bitcast(F32),
                                  ALU.subtract).then_inc(buf_lo_ready, 1)

            def low_hidden(e):
                for f in range(KF):
                    dve.wait_ge(hid_hi_ready, KF * e + f + 1)
                    dve.tensor_tensor(hid_lo[:, f], hid[:, f % 2], hid_hi[:, f].bitcast(F32),
                                      ALU.subtract).then_inc(hid_lo_ready, 1)
            base, LINKS = done[0], 7

            def take_results(e, b):
                dve.wait_ge(ffn_done, past(e + 1))
                dve.wait_ge(yb_free, e + 1)
                for j in range(4):
                    dve.tensor_tensor(yb[:, b, j], PS[0:SP4, 4 + j, 0:D], flat(b2row[:, one(e), :]),
                                      ALU.add).then_inc(y_copied, 1)

            def finish(e, i, b):
                n = 0

                def then(ins):
                    nonlocal n
                    n += 1
                    ins.then_inc(dve_step, 1)
                    hold(dve, dve_step, LINKS * e + (base + n))
                hold(dve, tail_ld[b], 16 * (i + 1))
                dve.tensor_copy(tok_i[:, b], tail[:, b, :, TOK - D])
                dve.wait_ge(y_copied, past(4 * e + 4))
                for j in range(4):
                    ins = dve.tensor_scalar(yb[:, b, j], yb[:, b, j], tail[:, b, j, PRB - D:PRB - D + 1], None,
                                            ALU.mult)
                then(ins)
                y = yb[:, b].rearrange("p j d -> p (j d)")
                then(dve.tensor_scalar(fin_a[:], y, FLT_MAX, None, ALU.is_le))
                then(dve.scalar_tensor_tensor(out=fin_b[:], in0=y, scalar=-FLT_MAX, in1=fin_a[:],
                                              op0=ALU.is_ge, op1=ALU.subtract))
                then(dve.tensor_scalar(fin_b[:], fin_b[:], INFINITE, None, ALU.mult))
                then(dve.scalar_tensor_tensor(out=fin_a[:].bitcast(I32), in0=y, scalar=-FLT_MAX, in1=fin_a[:],
                                              op0=ALU.is_ge, op1=ALU.mult))
                then(dve.copy_predicated(fin_b[:], fin_a[:].bitcast(I32), y))
                then(dve.tensor_tensor(yb[:, b], fin_b[:].rearrange("p (j d) -> p j d", j=4),
                                       tail[:, b, :, RES - D:ROW - D], ALU.add))
                dve.sem_inc(y_ready, 1)
                assert n == LINKS
            low_rows(0)
            low_hidden(0)
            low_rows(1)
            dve.wait_ge(b2_ld, 16)
            with dve.Fori(1, NX // 2) as i:
                take_results(2 * i - 2, 0)
                low_hidden(2 * i - 1)
                low_rows(2 * i)
                finish(2 * i - 2, i - 1, 0)
                take_results(2 * i - 1, 1)
                low_hidden(2 * i)
                low_rows(2 * i + 1)
                finish(2 * i - 1, i - 1, 1)
            take_results(NX - 2, 0)
            low_hidden(NX - 1)
            finish(NX - 2, NX // 2 - 1, 0)
            take_results(NX - 1, 1)
            finish(NX - 1, NX // 2 - 1, 1)


INPUTS = ["x", "src", "dst", "L0_gnn_conv_weight", "L0_gnn_conv_bias", "L0_gnn_self_weight", "L0_gnn_bias",
          "L0_gnn_gamma", "L0_gnn_beta", "L0_ffn_gate_w", "L0_ffn_gate_b", "L0_ffn_w1", "L0_ffn_b1",
          "L0_ffn_w2", "L0_ffn_b2"]


def kernel(**inputs):
    import numpy as np
    import concourse.bacc as bacc
    from concourse.bass_utils import run_bass_kernel_spmd

    nc = bacc.Bacc("TRN2", target_bir_lowering=False, num_devices=1)
    arrays, args = {}, []
    for name in INPUTS:
        a = np.ascontiguousarray(inputs[name])
        arrays[f"in_{name}"] = a
        args.append(nc.dram_tensor(f"in_{name}", a.shape, mybir.dt.from_np(a.dtype), kind="ExternalInput").ap())
    shape = arrays["in_x"].shape
    args.append(nc.dram_tensor("out", shape, F32, kind="ExternalOutput").ap())
    gnn_then_moe(nc, *args)
    r = run_bass_kernel_spmd(nc, [arrays], core_ids=[0])
    return r.results[0]["out"]
```
